# Optimizing a Trainium2 kernel written in Bass

```python
import numpy as np
import jax
import jax.numpy as jnp

def _softmax(x, axis=-1):
    return jax.nn.softmax(x, axis=axis)
def _gelu(x):
    return jax.nn.gelu(x, approximate=True)
def _silu(x):
    return jax.nn.silu(x)
def _sigmoid(x):
    return jax.nn.sigmoid(x)
def _layernorm(x, axis=-1, eps=1e-5):
    m = jnp.mean(x, axis=axis, keepdims=True)
    v = jnp.var(x, axis=axis, keepdims=True)
    return (x - m) / jnp.sqrt(v + eps)
def _scatter_add(tgt, idx, src, axis=0):
    return tgt.at[idx].add(src)
def _segment_sum(src, seg, n):
    return jax.ops.segment_sum(src, seg, n)

kernel_name = 'mk_conv_seq_d2_conv_nchw64_b81aa8'

def setup_inputs(seed: int = 0):
    np.random.seed(seed)
    _w = jnp.asarray
    def _rec_inputs():
        import jax
        import jax.numpy as jnp
        _gk = jax.random.key(seed)
        x = -9.26e-05 + 0.9999 * jax.random.normal(jax.random.fold_in(_gk, 1), (16, 64, 192, 192), jnp.float32)
        return x
    x = _rec_inputs()
    def _L0_conv_setup():
        import jax, jax.numpy as jnp
        import numpy as np
        K = 3
        PAD = 1
        GAIN = 1.4142135623730951
        STD_SPATIAL = GAIN / K
        EPS = 1e-10
        NEG_SLOPE = 0.1
        RES_SCALE = 1.0

        def _filter_norm_spatial(f):
            m = f.mean(axis=1, keepdims=True)
            s = f.std(axis=1, keepdims=True, ddof=1)
            return (f - m) / (s + EPS) * STD_SPATIAL

        def _filter_norm_channel(f, std_ch, C):
            B = f.shape[0]
            f = f.reshape(B, C, K * K)
            m = f.mean(axis=2, keepdims=True)
            s = f.std(axis=2, keepdims=True, ddof=1)
            f = (f - m) / (s + EPS)
            return f.reshape(B, -1) * std_ch

        def _ddf_mul(x, cf, sf):
            B, C, H, W = x.shape
            xp = jnp.pad(x, ((0, 0), (0, 0), (PAD, PAD), (PAD, PAD)))
            out = jnp.zeros_like(x)
            for t in range(K * K):
                u, v = (t // K, t % K)
                patch = xp[:, :, u:u + H, v:v + W]
                out = out + patch * cf[:, :, t, None, None] * sf[:, t:t + 1, :, :]
            return out

        def _ddfpack(x, Ws, bs, W1, b1, W2, b2, std_ch):
            B, C, H, W = x.shape
            sf = jnp.einsum('bchw,kc->bkhw', x, Ws) + bs[None, :, None, None]
            sf = _filter_norm_spatial(sf)
            pooled = x.mean(axis=(2, 3))
            h = jax.nn.relu(pooled @ W1.T + b1)
            cf = h @ W2.T + b2
            cf = _filter_norm_channel(cf, std_ch, C).reshape(B, C, K * K)
            return _ddf_mul(x, cf, sf)
        key = jax.random.key(seed)
        ks = jax.random.split(key, 10)
        B, C, H, W = (16, 64, 192, 192)
        mid = int(C * 0.2)
        return {'x': jax.random.normal(ks[0], (B, C, H, W), jnp.float32), 'Ws': jax.random.normal(ks[1], (K * K, C), jnp.float32) * 0.1, 'bs': jax.random.normal(ks[2], (K * K,), jnp.float32) * 0.1, 'W1': jax.random.normal(ks[3], (mid, C), jnp.float32) * 0.1, 'b1': jax.random.normal(ks[4], (mid,), jnp.float32) * 0.1, 'W2': jax.random.normal(ks[5], (C * K * K, mid), jnp.float32) * 0.1, 'b2': jax.random.normal(ks[6], (C * K * K,), jnp.float32) * 0.1, 'std_ch': jax.random.normal(ks[7], (C * K * K,), jnp.float32) * STD_SPATIAL, 'Wc': jax.random.normal(ks[8], (C, C, K, K), jnp.float32) * 0.05, 'bc': jax.random.normal(ks[9], (C,), jnp.float32) * 0.05}
    _L0_conv_all = _L0_conv_setup()
    _L0_conv_in = {k: v for k, v in _L0_conv_all.items() if k in ('Ws', 'bs', 'W1', 'b1', 'W2', 'b2', 'std_ch', 'Wc', 'bc', )}
    del _L0_conv_all

    def _L1_conv_setup():
        import jax, jax.numpy as jnp
        import numpy as np
        K = 3
        EPS = 1e-10

        def _filter_norm_spatial(s, std_param):
            s = s - s.mean(axis=1, keepdims=True)
            s = s / (s.std(axis=1, keepdims=True, ddof=1) + EPS)
            return s * std_param[None, :, None, None]

        def _filter_norm_channel(cf, std_param, B, C):
            cf = cf.reshape(B, C, K * K)
            cf = cf - cf.mean(axis=2, keepdims=True)
            cf = cf / (cf.std(axis=2, keepdims=True, ddof=1) + EPS)
            cf = cf.reshape(B, C * K * K) * std_param[None, :]
            return cf.reshape(B, C, K * K)

        def _ddf_pack(x, sw, sb, sstd, cw1, cb1, cw2, cb2, cstd):
            B, C, H, W = x.shape
            s = jnp.einsum('bchw,oc->bohw', x, sw) + sb[None, :, None, None]
            s = _filter_norm_spatial(s, sstd)
            g = x.mean(axis=(2, 3))
            h = jax.nn.relu(g @ cw1.T + cb1)
            cf = h @ cw2.T + cb2
            cf = _filter_norm_channel(cf, cstd, B, C)
            pad = K // 2
            xp = jnp.pad(x, ((0, 0), (0, 0), (pad, pad), (pad, pad)))
            patches = jnp.stack([xp[:, :, i:i + H, j:j + W] for i in range(K) for j in range(K)], axis=2)
            return jnp.einsum('bckhw,bck,bkhw->bchw', patches, cf, s)
        key = jax.random.key(seed)
        ks = jax.random.split(key, 20)
        nf, mid = (64, 12)
        std_scale = np.sqrt(2.0) / K
        d = {'x': jax.random.normal(ks[0], (4, nf, 256, 256), jnp.float32)}
        i = 1
        for p in ('1', '2'):
            d['sw' + p] = jax.random.normal(ks[i], (K * K, nf), jnp.float32) * 0.1
            i += 1
            d['sb' + p] = jax.random.normal(ks[i], (K * K,), jnp.float32) * 0.1
            i += 1
            d['sstd' + p] = jax.random.normal(ks[i], (K * K,), jnp.float32) * std_scale
            i += 1
            d['cw1_' + p] = jax.random.normal(ks[i], (mid, nf), jnp.float32) * 0.1
            i += 1
            d['cb1_' + p] = jax.random.normal(ks[i], (mid,), jnp.float32) * 0.1
            i += 1
            d['cw2_' + p] = jax.random.normal(ks[i], (nf * K * K, mid), jnp.float32) * 0.1
            i += 1
            d['cb2_' + p] = jax.random.normal(ks[i], (nf * K * K,), jnp.float32) * 0.1
            i += 1
            d['cstd' + p] = jax.random.normal(ks[i], (nf * K * K,), jnp.float32) * std_scale
            i += 1
        return d
    _L1_conv_all = _L1_conv_setup()
    _L1_conv_in = {k: v for k, v in _L1_conv_all.items() if k in ('sw1', 'sb1', 'sstd1', 'cw1_1', 'cb1_1', 'cw2_1', 'cb2_1', 'cstd1', 'sw2', 'sb2', 'sstd2', 'cw1_2', 'cb1_2', 'cw2_2', 'cb2_2', 'cstd2', )}
    del _L1_conv_all

    return {
        "x": x,
        "L0_conv_Ws": _L0_conv_in["Ws"],
        "L0_conv_bs": _L0_conv_in["bs"],
        "L0_conv_W1": _L0_conv_in["W1"],
        "L0_conv_b1": _L0_conv_in["b1"],
        "L0_conv_W2": _L0_conv_in["W2"],
        "L0_conv_b2": _L0_conv_in["b2"],
        "L0_conv_std_ch": _L0_conv_in["std_ch"],
        "L0_conv_Wc": _L0_conv_in["Wc"],
        "L0_conv_bc": _L0_conv_in["bc"],
        "L1_conv_sw1": _L1_conv_in["sw1"],
        "L1_conv_sb1": _L1_conv_in["sb1"],
        "L1_conv_sstd1": _L1_conv_in["sstd1"],
        "L1_conv_cw1_1": _L1_conv_in["cw1_1"],
        "L1_conv_cb1_1": _L1_conv_in["cb1_1"],
        "L1_conv_cw2_1": _L1_conv_in["cw2_1"],
        "L1_conv_cb2_1": _L1_conv_in["cb2_1"],
        "L1_conv_cstd1": _L1_conv_in["cstd1"],
        "L1_conv_sw2": _L1_conv_in["sw2"],
        "L1_conv_sb2": _L1_conv_in["sb2"],
        "L1_conv_sstd2": _L1_conv_in["sstd2"],
        "L1_conv_cw1_2": _L1_conv_in["cw1_2"],
        "L1_conv_cb1_2": _L1_conv_in["cb1_2"],
        "L1_conv_cw2_2": _L1_conv_in["cw2_2"],
        "L1_conv_cb2_2": _L1_conv_in["cb2_2"],
        "L1_conv_cstd2": _L1_conv_in["cstd2"],
    }

def reference(x, L0_conv_Ws, L0_conv_bs, L0_conv_W1, L0_conv_b1, L0_conv_W2, L0_conv_b2, L0_conv_std_ch, L0_conv_Wc, L0_conv_bc, L1_conv_sw1, L1_conv_sb1, L1_conv_sstd1, L1_conv_cw1_1, L1_conv_cb1_1, L1_conv_cw2_1, L1_conv_cb2_1, L1_conv_cstd1, L1_conv_sw2, L1_conv_sb2, L1_conv_sstd2, L1_conv_cw1_2, L1_conv_cb1_2, L1_conv_cw2_2, L1_conv_cb2_2, L1_conv_cstd2):
    import jax
    import jax.numpy as jnp
    def _L0_conv_ref(x, Ws, bs, W1, b1, W2, b2, std_ch, Wc, bc):
        import jax, jax.numpy as jnp
        import numpy as np
        K = 3
        PAD = 1
        GAIN = 1.4142135623730951
        STD_SPATIAL = GAIN / K
        EPS = 1e-10
        NEG_SLOPE = 0.1
        RES_SCALE = 1.0

        def _filter_norm_spatial(f):
            m = f.mean(axis=1, keepdims=True)
            s = f.std(axis=1, keepdims=True, ddof=1)
            return (f - m) / (s + EPS) * STD_SPATIAL

        def _filter_norm_channel(f, std_ch, C):
            B = f.shape[0]
            f = f.reshape(B, C, K * K)
            m = f.mean(axis=2, keepdims=True)
            s = f.std(axis=2, keepdims=True, ddof=1)
            f = (f - m) / (s + EPS)
            return f.reshape(B, -1) * std_ch

        def _ddf_mul(x, cf, sf):
            B, C, H, W = x.shape
            xp = jnp.pad(x, ((0, 0), (0, 0), (PAD, PAD), (PAD, PAD)))
            out = jnp.zeros_like(x)
            for t in range(K * K):
                u, v = (t // K, t % K)
                patch = xp[:, :, u:u + H, v:v + W]
                out = out + patch * cf[:, :, t, None, None] * sf[:, t:t + 1, :, :]
            return out

        def _ddfpack(x, Ws, bs, W1, b1, W2, b2, std_ch):
            B, C, H, W = x.shape
            sf = jnp.einsum('bchw,kc->bkhw', x, Ws) + bs[None, :, None, None]
            sf = _filter_norm_spatial(sf)
            pooled = x.mean(axis=(2, 3))
            h = jax.nn.relu(pooled @ W1.T + b1)
            cf = h @ W2.T + b2
            cf = _filter_norm_channel(cf, std_ch, C).reshape(B, C, K * K)
            return _ddf_mul(x, cf, sf)
        out = _ddfpack(x, Ws, bs, W1, b1, W2, b2, std_ch)
        out = jnp.where(out >= 0, out, NEG_SLOPE * out)
        out = jax.lax.conv_general_dilated(out, Wc, window_strides=(1, 1), padding='SAME', dimension_numbers=('NCHW', 'OIHW', 'NCHW'))
        out = out + bc[None, :, None, None]
        return x + out * RES_SCALE

    def _L1_conv_ref(x, sw1, sb1, sstd1, cw1_1, cb1_1, cw2_1, cb2_1, cstd1, sw2, sb2, sstd2, cw1_2, cb1_2, cw2_2, cb2_2, cstd2):
        import jax, jax.numpy as jnp
        import numpy as np
        K = 3
        EPS = 1e-10

        def _filter_norm_spatial(s, std_param):
            s = s - s.mean(axis=1, keepdims=True)
            s = s / (s.std(axis=1, keepdims=True, ddof=1) + EPS)
            return s * std_param[None, :, None, None]

        def _filter_norm_channel(cf, std_param, B, C):
            cf = cf.reshape(B, C, K * K)
            cf = cf - cf.mean(axis=2, keepdims=True)
            cf = cf / (cf.std(axis=2, keepdims=True, ddof=1) + EPS)
            cf = cf.reshape(B, C * K * K) * std_param[None, :]
            return cf.reshape(B, C, K * K)

        def _ddf_pack(x, sw, sb, sstd, cw1, cb1, cw2, cb2, cstd):
            B, C, H, W = x.shape
            s = jnp.einsum('bchw,oc->bohw', x, sw) + sb[None, :, None, None]
            s = _filter_norm_spatial(s, sstd)
            g = x.mean(axis=(2, 3))
            h = jax.nn.relu(g @ cw1.T + cb1)
            cf = h @ cw2.T + cb2
            cf = _filter_norm_channel(cf, cstd, B, C)
            pad = K // 2
            xp = jnp.pad(x, ((0, 0), (0, 0), (pad, pad), (pad, pad)))
            patches = jnp.stack([xp[:, :, i:i + H, j:j + W] for i in range(K) for j in range(K)], axis=2)
            return jnp.einsum('bckhw,bck,bkhw->bchw', patches, cf, s)
        out = _ddf_pack(x, sw1, sb1, sstd1, cw1_1, cb1_1, cw2_1, cb2_1, cstd1)
        out = jax.nn.relu(out)
        out = _ddf_pack(out, sw2, sb2, sstd2, cw1_2, cb1_2, cw2_2, cb2_2, cstd2)
        return x + out

    def _gn(v, G=32, eps=1e-5):
        B_, C_, H_, W_ = v.shape
        g = v.reshape(B_, G, C_ // G, H_, W_)
        m = jnp.mean(g, axis=(2, 3, 4), keepdims=True)
        s = jnp.var(g, axis=(2, 3, 4), keepdims=True)
        return ((g - m) / jnp.sqrt(s + eps)).reshape(v.shape)

    def _ln_c(v, eps=1e-6):
        m = jnp.mean(v, axis=1, keepdims=True)
        s = jnp.var(v, axis=1, keepdims=True)
        return (v - m) / jnp.sqrt(s + eps)

    def _ln_t(v, eps=1e-5):
        m = jnp.mean(v, axis=-1, keepdims=True)
        s = jnp.var(v, axis=-1, keepdims=True)
        return (v - m) / jnp.sqrt(s + eps)

    def _to_tokens(v):
        B_, C_, H_, W_ = v.shape
        return v.reshape(B_, C_, H_ * W_).transpose(0, 2, 1)
    def _from_tokens(t, like):
        B_, C_, H_, W_ = like.shape
        return t.transpose(0, 2, 1).reshape(B_, C_, H_, W_)

    x = _L0_conv_ref(x, L0_conv_Ws, L0_conv_bs, L0_conv_W1, L0_conv_b1, L0_conv_W2, L0_conv_b2, L0_conv_std_ch, L0_conv_Wc, L0_conv_bc)
    x = _L1_conv_ref(x, L1_conv_sw1, L1_conv_sb1, L1_conv_sstd1, L1_conv_cw1_1, L1_conv_cb1_1, L1_conv_cw2_1, L1_conv_cb2_1, L1_conv_cstd1, L1_conv_sw2, L1_conv_sb2, L1_conv_sstd2, L1_conv_cw1_2, L1_conv_cb1_2, L1_conv_cw2_2, L1_conv_cb2_2, L1_conv_cstd2)
    return x


_drawn_inputs = setup_inputs


def setup_inputs(seed=0):
    import zlib

    import numpy as np

    out = dict(_drawn_inputs(seed))
    spreads = {}
    factors = {'L0_conv_W1': 8.0}
    for name, (base, spread) in spreads.items():
        noise = np.random.default_rng([zlib.crc32(name.encode()), seed]).standard_normal(out[name].shape)
        drawn = base * np.exp(spread * noise) if base else spread * noise
        out[name] = jnp.asarray(drawn.astype(out[name].dtype))
    for name, factor in factors.items():
        out[name] = (out[name] * factor).astype(out[name].dtype)
    return out
```

```python
from contextlib import ExitStack

import numpy as np

import concourse.bass as bass
from concourse import mybir

F32 = mybir.dt.float32
BF16 = mybir.dt.bfloat16
ALU = mybir.AluOpType
ACT = mybir.ActivationFunctionType
AX_X = mybir.AxisListType.X
ds = bass.ds

IMAGES, C, H, W = 16, 64, 192, 192
TAPS, MID = 9, 12
P = 128
HALVES = 2
HROWS = H // HALVES
PITCH = W + 1
IMG = (HROWS + 2) * PITCH + 2
ROWS = 4
TILE = ROWS * W
TILES = HROWS // ROWS
CHUNK = TILE // 2
PPITCH = 256
PARTS = 3
FILTERS = PARTS * HALVES * TAPS
DDFS = 3
PER_IMAGE = DDFS * TILES
PIECE_ENDS = (24, 48, 72, 88, 96)
PIECES = len(PIECE_ENDS)
PIECE_STARTS = (0,) + PIECE_ENDS[:-1]
SLOPE = 0.1
EPS = 1e-10
TINY = 2.0 ** -63
STD_SPATIAL = 1.4142135623730951 / 3

CF_STEPS = 9
PRIMED = 1

RESIDUAL = "residual"
ADDED = ((1, 2, 3, 4, 5, 6, 7), (1, 3, 4, 6, 7), (RESIDUAL, 1, 3, 4, 6, 7))
SLOTS = ({1: 2, 2: 3, 3: 4, 4: 5, 5: 6, 6: 7, 7: 8}, {1: 2, 3: 3, 4: 4, 6: 2, 7: 3, 5: 7, 8: 8})
TAP2_SLOTS = (5, 6)
ADDS = tuple(len(a) for a in ADDED)
CONV_SUMS = HROWS // 2 + 1
CONV_GROUPS = HROWS // 2


def ddf_stack_kernel(nc, x, wspatial_in, bspatial_in, w1_in, b1_in, w2_in, tabs_in, wconv_in, bconv_in,
                     ident_in, wvar_in, wcopy_in, masks_in, out):
    ctx = ExitStack()
    with ctx:
        def sb(name, shape, dt=F32):
            return ctx.enter_context(nc.sbuf_tensor(name, shape, dt))

        def pb(name, shape):
            return ctx.enter_context(nc.psum_tensor(name, shape, F32))

        def sem(name):
            return ctx.enter_context(nc.semaphore(name))

        img_a = sb("img_a", [P, IMG])
        img_b = sb("img_b", [P, IMG])
        prod = sb("prod", [P, 9, TILE])
        wcopy_f32 = prod[:, 0:3, :].rearrange("p a n -> p (a n)")
        result = sb("result", [P, 2, TILE])
        squares = sb("squares", [P, CHUNK])
        rstd = sb("rstd", [P, CHUNK])
        normed = sb("normed", [P, CHUNK])
        high = sb("high", [P, CHUNK], BF16)
        rest = squares
        middle = sb("middle", [P, CHUNK], BF16)
        filters = sb("filters", [P, 2, CHUNK], BF16)
        wfilt = sb("wfilt", [P, DDFS, 2, P])
        wvar = sb("wvar", [P, P])
        ident = sb("ident", [P, P])
        wcopy = sb("wcopy", [P, 2 * TAPS, P], BF16)
        wconv = sb("wconv", [P, TAPS, P])
        bconv = sb("bconv", [P, 1])
        w1 = sb("w1", [P, DDFS, 32])
        b1 = sb("b1", [32 * DDFS, 1])
        w2 = sb("w2", [32 * DDFS, TAPS, P])
        tabs = sb("tabs", [P, 3, DDFS, TAPS])
        masks = sb("masks", [P, 4])
        wspatial = sb("wspatial", [P, DDFS, TAPS])
        wmean = sb("wmean", [P, DDFS])
        bspatial = sb("bspatial", [1, DDFS, TAPS])
        bmean = sb("bmean", [1, DDFS])
        brow = prod[0:1, 8, 0:DDFS * P].rearrange("p (d m) -> p d m", d=DDFS)
        bcol = sb("bcol", [P, DDFS])
        sums = sb("sums", [P, CONV_SUMS])
        pooled = sb("pooled", [P, 1])
        hidden = sb("hidden", [32 * DDFS, 1])
        cf_raw = sb("cf_raw", [P, TAPS])
        cf_mean = sb("cf_mean", [P, 1])
        cf_sq = sb("cf_sq", [P, TAPS])
        cf_var = sb("cf_var", [P, 1])
        cf_std = sb("cf_std", [P, 1])
        cf_inv = sb("cf_inv", [P, 1])
        cf = sb("cf", [P, TAPS])

        spread = [pb(f"spread{i}", [P, ROWS * PPITCH]) for i in range(2)]
        acc = pb("acc", [P, ROWS * PPITCH])
        p_filt = pb("p_filt", [P, 512])
        p_var = pb("p_var", [P, 512])

        consts_in = sem("consts_in")
        zeroed = sem("zeroed")
        prep = sem("prep")
        bias_rows = sem("bias_rows")
        bias_psum = sem("bias_psum")
        weights_ready = sem("weights_ready")
        x_in = [sem(f"x_in{i}") for i in range(PIECES)]
        x_summed = sem("x_summed")
        halo_a = sem("halo_a")
        halo_b = sem("halo_b")
        filt_ready = sem("filt_ready")
        squares_ready = sem("squares_ready")
        var_ready = sem("var_ready")
        inv_step = sem("inv_step")
        normed_ready = sem("normed_ready")
        high_ready = sem("high_ready")
        rest_ready = sem("rest_ready")
        middle_ready = sem("middle_ready")
        split_ready = sem("split_ready")
        spread_ready = sem("spread_ready")
        product_ready = sem("product_ready")
        sum_step = sem("sum_step")
        acc_ready = sem("acc_ready")
        total_ready = sem("total_ready")
        tile_done = sem("tile_done")
        conv_ready = sem("conv_ready")
        conv_stored = sem("conv_stored")
        pooled_ready = sem("pooled_ready")
        hidden_psum = sem("hidden_psum")
        hidden_ready = sem("hidden_ready")
        cf_psum = sem("cf_psum")
        cf_step = sem("cf_step")
        cf_std_step = sem("cf_std_step")
        stored = [sem(f"stored{i}") for i in range(2)]

        def added(im, ddf, i=0):
            return im * (TILES * sum(ADDS)) + (TILES * sum(ADDS[:ddf]) + PRIMED) + i * ADDS[ddf]

        def rows(img, r, count, dv):
            return img[:, ds(r * PITCH + dv, count * PITCH)].rearrange("p (r w) -> p r w", w=PITCH)[:, :, 0:W]

        def psum_rows(t, r=0, count=ROWS):
            return t[:, r * PPITCH:(r + count) * PPITCH].rearrange("p (r w) -> p r w", w=PPITCH)[:, :, 0:W]

        def flat(t):
            return t.rearrange("p (r w) -> p r w", w=W)

        def tiles(eng, step):
            step(0, 0, 0, edge=True)
            step(1, 0, 1, edge=True)
            with eng.Fori(1, TILES // 2 - 1) as pair:
                step(2 * pair, pair, 0)
                step(2 * pair + 1, pair, 1)
            step(TILES - 2, TILES // 2 - 1, 0)
            step(TILES - 1, TILES // 2 - 1, 1, last=True)

        source = (img_a, img_a, img_b)

        block = ctx.enter_context(nc.Block())

        @block.sync
        def _(sp):
            for primed in (normed_ready, product_ready, sum_step, tile_done, *stored):
                sp.sem_inc(primed, PRIMED)
            for dst, src in ((wspatial[:], wspatial_in), (bspatial[:], bspatial_in), (w1[:], w1_in), (b1[:], b1_in),
                             (w2[:], w2_in), (tabs[:], tabs_in), (wconv[:], wconv_in), (bconv[:], bconv_in),
                             (ident[:], ident_in), (wvar[:], wvar_in), (wcopy_f32, wcopy_in), (masks[:], masks_in)):
                sp.dma_start(dst, src).then_inc(consts_in, 16)

            def load(image, piece):
                for half in range(HALVES):
                    lo, hi = PIECE_STARTS[piece], PIECE_ENDS[piece]
                    if half == 0 and piece == PIECES - 1:
                        hi += 1
                    if half == 1 and piece == 0:
                        lo -= 1
                    g = half * HROWS
                    dst = img_a[half * C:(half + 1) * C, (lo + 1) * PITCH + 1:(hi + 1) * PITCH + 1]
                    sp.dma_start(dst.rearrange("p (r w) -> p r w", w=PITCH)[:, :, 0:W],
                                 x[ds(image, 1), :, g + lo:g + hi, :].rearrange("b c r w -> (b c) r w"))\
                      .then_inc(x_in[piece], 16)

            def image_body(im, load_next):
                for img, done, count, signal in (
                        (img_b, tile_done, im * PER_IMAGE + TILES + PRIMED, halo_b),
                        (img_a, conv_stored, im * CONV_SUMS + CONV_SUMS, halo_a),
                        (img_b, tile_done, im * PER_IMAGE + 2 * TILES + PRIMED, halo_b)):
                    sp.wait_ge(done, count)
                    sp.dma_start(img[0:C, (HROWS + 1) * PITCH + 1:(HROWS + 1) * PITCH + 1 + W],
                                 img[C:P, PITCH + 1:PITCH + 1 + W]).then_inc(signal, 16)
                    sp.dma_start(img[C:P, 1:1 + W],
                                 img[0:C, HROWS * PITCH + 1:HROWS * PITCH + 1 + W]).then_inc(signal, 16)

                def store(i, par):
                    sp.wait_ge(tile_done, im * PER_IMAGE + 2 * TILES + i + 1 + PRIMED)
                    for half in range(HALVES):
                        dst = out[ds(im, 1), :, ds(i * ROWS + half * HROWS, ROWS), :]
                        sp.dma_start(dst.rearrange("b c r w -> (b c) (r w)"),
                                     result[half * C:(half + 1) * C, par, :]).then_inc(stored[par], 16)

                for piece in range(PIECES):
                    with sp.Fori(PIECE_STARTS[piece] // ROWS // 2, PIECE_ENDS[piece] // ROWS // 2) as pair:
                        store(2 * pair, 0)
                        store(2 * pair + 1, 1)
                    if load_next:
                        load(im + 1, piece)

            sp.wait_ge(zeroed, 2)
            for piece in range(PIECES):
                load(0, piece)
            with sp.Fori(0, IMAGES - 1) as im:
                image_body(im, True)
            image_body(IMAGES - 1, False)
            for par in range(2):
                sp.wait_ge(stored[par], IMAGES * TILES // 2 * HALVES * 16 + PRIMED)

        @block.gpsimd
        def _(pool):
            nc.gpsimd.memset(img_a[:, :], 0.0).then_inc(zeroed, 1)
            pool.wait_ge(weights_ready, 1)

            with pool.Fori(0, IMAGES) as im:
                for ddf in range(DDFS):
                    base = im * PER_IMAGE + ddf * TILES

                    def step(i, par, ddf=ddf, base=base):
                        total = prod[:, par, :]
                        for k, tap in enumerate(ADDED[ddf]):
                            if tap == RESIDUAL:
                                pool.wait_ge(product_ready, (base + i) * TAPS + 1 + PRIMED)
                                nc.gpsimd.tensor_tensor(out=flat(total), in0=flat(total),
                                                        in1=rows(img_a, i * ROWS + 1, ROWS, 1),
                                                        op=ALU.add).then_inc(sum_step, 1)
                                continue
                            pool.wait_ge(product_ready, (base + i) * TAPS + tap + 1 + PRIMED)
                            if k:
                                pool.wait_ge(sum_step, added(im, ddf, i) + k)
                            nc.gpsimd.tensor_tensor(out=total, in0=total, in1=prod[:, SLOTS[ddf > 0][tap], :],
                                                    op=ALU.add).then_inc(sum_step, 1)

                    with pool.Fori(0, TILES // 2) as pair:
                        step(2 * pair, 0)
                        step(2 * pair + 1, 1)

        @block.scalar
        def _(act):
            nc.scalar.preload_act_table_set("natural_log_exp_and_others")
            act.wait_ge(weights_ready, 1)

            def invert(m, ddf):
                act.wait_ge(filt_ready, m + 1)
                nc.scalar.activation(squares[:], p_filt[:, 0:CHUNK], ACT.Square,
                                     bias=bcol[:, ddf:ddf + 1]).then_inc(squares_ready, 1)
                act.wait_ge(var_ready, m + 1)
                act.wait_ge(normed_ready, m + PRIMED)
                nc.scalar.activation(rstd[:], p_var[:, 0:CHUNK], ACT.Ln, bias=masks[:, 3:4]).then_inc(inv_step, 1)
                act.wait_ge(inv_step, 4 * m + 1)
                nc.scalar.activation(rstd[:], rstd[:], ACT.Exp, scale=0.5).then_inc(inv_step, 1)
                act.wait_ge(inv_step, 4 * m + 2)
                nc.scalar.activation(rstd[:], rstd[:], ACT.Ln, bias=masks[:, 2:3]).then_inc(inv_step, 1)
                act.wait_ge(inv_step, 4 * m + 3)
                nc.scalar.activation(rstd[:], rstd[:], ACT.Exp, scale=-1.0).then_inc(inv_step, 1)

            def round_parts(m):
                act.wait_ge(normed_ready, m + 1 + PRIMED)
                nc.scalar.activation(high[:], normed[:], ACT.Copy).then_inc(high_ready, 1)
                act.wait_ge(rest_ready, m + 1)
                nc.scalar.activation(middle[:], rest[:], ACT.Copy).then_inc(middle_ready, 1)

            with act.Fori(0, IMAGES) as im:
                for piece in range(PIECES):
                    act.wait_ge(x_in[piece], (im + 1) * HALVES * 16)
                    v = img_a[:, (PIECE_STARTS[piece] + 1) * PITCH + 1:(PIECE_ENDS[piece] + 1) * PITCH + 1]
                    nc.scalar.activation(v, v, ACT.Copy, accum_out=sums[:, piece:piece + 1]).then_inc(x_summed, 1)
                for ddf in range(DDFS):
                    base = im * PER_IMAGE + ddf * TILES
                    invert(base, ddf)
                    round_parts(base)
                    q = slice(32 * ddf, 32 * ddf + 32)
                    act.wait_ge(hidden_psum, im * DDFS + ddf + 1)
                    nc.scalar.activation(hidden[q, :], acc[q, 0:1], ACT.Relu, bias=b1[q, :],
                                         scale=1.0 / (H * W)).then_inc(hidden_ready, 1)
                    act.wait_ge(cf_step, (im * DDFS + ddf) * CF_STEPS + 6)
                    nc.scalar.activation(cf_std[:], cf_var[:], ACT.Ln, bias=masks[:, 3:4],
                                         scale=1.0 / (TAPS - 1)).then_inc(cf_std_step, 1)
                    act.wait_ge(cf_std_step, (im * DDFS + ddf) * 2 + 1)
                    nc.scalar.activation(cf_std[:], cf_std[:], ACT.Exp, scale=0.5).then_inc(cf_std_step, 1)

                    def finish(i, pair, par, ddf=ddf, base=base):
                        if ddf == 2:
                            act.wait_ge(stored[par], (im * (TILES // 2) + pair) * (HALVES * 16) + PRIMED)
                        act.wait_ge(acc_ready, im * (2 * TILES) + (ddf - 1) * TILES + i + 1)
                        if ddf == 1:
                            nc.scalar.activation(rows(img_b, i * ROWS + 1, ROWS, 1), psum_rows(acc), ACT.Relu,
                                                 accum_out=sums[:, ds(i, 1)]).then_inc(tile_done, 1)
                        else:
                            nc.scalar.activation(flat(result[:, par, :]), psum_rows(acc),
                                                 ACT.Copy).then_inc(tile_done, 1)

                    def step(i, pair, par, edge=False, last=False, ddf=ddf, base=base, finish=finish):
                        if ddf and not edge:
                            finish(i - 2, pair - 1, par)
                        if not last:
                            invert(base + i + 1, ddf)
                            round_parts(base + i + 1)

                    tiles(act, step)
                    if ddf:
                        finish(TILES - 2, TILES // 2 - 1, 0)
                        finish(TILES - 1, TILES // 2 - 1, 1)

        @block.vector
        def _(dve):
            nc.vector.memset(img_b[:, :], 0.0).then_inc(zeroed, 1)
            nc.vector.memset(wfilt[:], 0.0).then_inc(prep, 1)
            nc.vector.memset(brow, 1.0).then_inc(prep, 1)
            dve.wait_ge(consts_in, 12 * 16)
            nc.vector.tensor_reduce(wmean[:], wspatial[:], AX_X, ALU.add).then_inc(prep, 1)
            nc.vector.tensor_reduce(bmean[:], bspatial[:], AX_X, ALU.add).then_inc(prep, 1)
            dve.wait_ge(prep, 4)
            nc.vector.tensor_scalar(wmean[:], wmean[:], -1.0 / TAPS, None, ALU.mult).then_inc(prep, 1)
            nc.vector.tensor_scalar(bmean[:], bmean[:], -1.0 / TAPS, None, ALU.mult).then_inc(prep, 1)
            dve.wait_ge(prep, 6)
            for d in range(DDFS):
                nc.vector.tensor_scalar(wspatial[:, d, :], wspatial[:, d, :], wmean[:, d:d + 1], None,
                                        ALU.add).then_inc(prep, 1)
                nc.vector.tensor_scalar(bspatial[:, d, :], bspatial[:, d, :], bmean[:, d:d + 1], None,
                                        ALU.add).then_inc(prep, 1)
            dve.wait_ge(prep, 6 + 2 * DDFS)
            for d in range(DDFS):
                for chunk in range(2):
                    for part in range(PARTS):
                        for half in range(HALVES):
                            at = (part * HALVES + half) * TAPS
                            h = slice(half * C, (half + 1) * C)
                            nc.vector.tensor_copy(wfilt[h, d, chunk, chunk * 64 + at:chunk * 64 + at + TAPS],
                                                  wspatial[h, d, :]).then_inc(prep, 1)
                            nc.vector.tensor_copy(brow[:, d, chunk * 64 + at:chunk * 64 + at + TAPS],
                                                  bspatial[:, d, :]).then_inc(bias_rows, 1)
            nc.vector.tensor_copy(wcopy[:].rearrange("p a n -> p (a n)"), wcopy_f32).then_inc(prep, 1)
            nc.vector.tensor_tensor(out=tabs[:, 1], in0=tabs[:, 1], in1=tabs[:, 2], op=ALU.mult).then_inc(prep, 1)
            dve.wait_ge(bias_psum, 1)
            nc.vector.tensor_copy(bcol[:], p_filt[:, 0:DDFS]).then_inc(prep, 1)
            dve.wait_ge(prep, 6 + 2 * DDFS + DDFS * 2 * PARTS * HALVES + 3)
            nc.vector.memset(sums[:], 0.0).then_inc(weights_ready, 1)
            dve.wait_ge(weights_ready, 1)

            def normalise(m, ddf):
                dve.wait_ge(inv_step, 4 * m + 4)
                nc.vector.scalar_tensor_tensor(out=normed[:], in0=p_filt[:, 0:CHUNK], scalar=bcol[:, ddf:ddf + 1],
                                               in1=rstd[:], op0=ALU.add, op1=ALU.mult).then_inc(normed_ready, 1)

            def take_high(m):
                dve.wait_ge(high_ready, m + 1)
                nc.vector.scalar_tensor_tensor(out=rest[:], in0=high[:], scalar=masks[:, 0:1], in1=normed[:],
                                               op0=ALU.mult, op1=ALU.add).then_inc(rest_ready, 1)

            def take_middle(m, par):
                dve.wait_ge(middle_ready, m + 1)
                nc.vector.scalar_tensor_tensor(out=filters[:, par, :], in0=middle[:], scalar=masks[:, 1:2],
                                               in1=rest[:], op0=ALU.mult, op1=ALU.add).then_inc(split_ready, 1)

            with dve.Fori(0, IMAGES) as im:

                def total(i, par):
                    dve.wait_ge(sum_step, added(im, 0, i) + ADDS[0])
                    nc.vector.tensor_tensor(out=result[:, par, :], in0=prod[:, par, :], in1=result[:, par, :],
                                            op=ALU.add).then_inc(total_ready, 1)

                def leaky(i, par):
                    dve.wait_ge(total_ready, im * TILES + i + 1)
                    nc.vector.scalar_tensor_tensor(out=rows(img_b, i * ROWS + 1, ROWS, 1), in0=flat(result[:, par, :]),
                                                   scalar=SLOPE, in1=flat(result[:, par, :]), op0=ALU.mult,
                                                   op1=ALU.max).then_inc(tile_done, 1)

                def conv_store(group, r, count, bank, column, wait=True):
                    if wait:
                        dve.wait_ge(conv_ready, im * CONV_GROUPS + group + 1)
                    nc.vector.scalar_tensor_tensor(out=rows(img_a, r + 1, count, 1), in0=psum_rows(acc, bank, count),
                                                   scalar=bconv[:, 0:1], in1=rows(img_a, r + 1, count, 1),
                                                   op0=ALU.add, op1=ALU.add,
                                                   accum_out=sums[:, ds(column, 1)]).then_inc(conv_stored, 1)

                for ddf in range(DDFS):
                    base = im * PER_IMAGE + ddf * TILES
                    done, count = ((x_summed, im * PIECES + PIECES), (conv_stored, im * CONV_SUMS + CONV_SUMS),
                                   (tile_done, im * PER_IMAGE + 2 * TILES + PRIMED))[ddf]
                    dve.wait_ge(done, count)
                    nc.vector.tensor_reduce(pooled[:], sums[:, 0:(PIECES, CONV_SUMS, TILES)[ddf]], AX_X,
                                            ALU.add).then_inc(pooled_ready, 1)
                    normalise(base, ddf)
                    take_high(base)
                    take_middle(base, 0)
                    at = (im * DDFS + ddf) * CF_STEPS
                    dve.wait_ge(cf_psum, im * DDFS + ddf + 1)
                    nc.vector.tensor_tensor(out=cf_raw[:], in0=acc[:, 512:512 + TAPS], in1=tabs[:, 0, ddf, :],
                                            op=ALU.add).then_inc(cf_step, 1)
                    dve.wait_ge(cf_step, at + 1)
                    nc.vector.tensor_reduce(cf_mean[:], cf_raw[:], AX_X, ALU.add).then_inc(cf_step, 1)
                    dve.wait_ge(cf_step, at + 2)
                    nc.vector.tensor_scalar(cf_mean[:], cf_mean[:], -1.0 / TAPS, None, ALU.mult).then_inc(cf_step, 1)
                    dve.wait_ge(cf_step, at + 3)
                    nc.vector.tensor_scalar(cf_raw[:], cf_raw[:], cf_mean[:, 0:1], None, ALU.add).then_inc(cf_step, 1)
                    dve.wait_ge(cf_step, at + 4)
                    nc.vector.tensor_tensor(out=cf_sq[:], in0=cf_raw[:], in1=cf_raw[:],
                                            op=ALU.mult).then_inc(cf_step, 1)
                    dve.wait_ge(cf_step, at + 5)
                    nc.vector.tensor_reduce(cf_var[:], cf_sq[:], AX_X, ALU.add).then_inc(cf_step, 1)
                    dve.wait_ge(cf_std_step, (im * DDFS + ddf) * 2 + 2)
                    nc.vector.tensor_scalar(cf_std[:], cf_std[:], EPS, None, ALU.add).then_inc(cf_step, 1)
                    dve.wait_ge(cf_step, at + 7)
                    nc.vector.reciprocal(cf_inv[:], cf_std[:]).then_inc(cf_step, 1)
                    dve.wait_ge(cf_step, at + 8)
                    nc.vector.scalar_tensor_tensor(out=cf[:], in0=cf_raw[:], scalar=cf_inv[:, 0:1],
                                                   in1=tabs[:, 1, ddf, :], op0=ALU.mult,
                                                   op1=ALU.mult).then_inc(cf_step, 1)
                    dve.wait_ge(cf_step, at + 9)
                    if ddf:
                        dve.wait_ge((halo_a, halo_b)[ddf - 1], im * (32 * ddf) + 32 * ddf)
                    if ddf == 0:
                        for par in range(2):
                            dve.wait_ge(stored[par], im * (TILES // 2 * HALVES * 16) + PRIMED)

                    def step(i, pair, par, edge=False, last=False, ddf=ddf, base=base):
                        n = base + i
                        first = edge and par == 0
                        for tap in range(TAPS):
                            if tap == 0:
                                dst = prod[:, par, :]
                            elif tap == 2 and ddf:
                                dst = prod[:, TAP2_SLOTS[par], :]
                            elif tap == 8 and ddf == 0:
                                dst = result[:, par, :]
                            else:
                                dst = prod[:, SLOTS[ddf > 0][tap], :]
                            if ddf == 0 and 1 <= tap <= 7 and not first:
                                dve.wait_ge(sum_step, added(im, ddf, i - 1) + tap)
                            if ddf and tap in (1, 3, 4) and not first:
                                dve.wait_ge(sum_step, added(im, ddf, i - 1) + ADDED[ddf].index({1: 6, 3: 7, 4: 4}[tap]) + 1)
                            if ddf and tap in (6, 7):
                                dve.wait_ge(sum_step, added(im, ddf, i) + ADDED[ddf].index({6: 1, 7: 3}[tap]) + 1)
                            dve.wait_ge(spread_ready, n * TAPS + tap + 1)
                            nc.vector.scalar_tensor_tensor(
                                out=flat(dst), in0=rows(source[ddf], i * ROWS + tap // 3, ROWS, tap % 3),
                                scalar=cf[:, tap:tap + 1], in1=psum_rows(spread[(par + tap) % 2]),
                                op0=ALU.mult, op1=ALU.mult).then_inc(product_ready, 1)
                            if ddf == 0 and not first:
                                if tap == 1:
                                    total(i - 1, 1 - par)
                                if tap == 2:
                                    leaky(i - 1, 1 - par)
                            if ddf == 0 and not edge and tap in (6, 8):
                                k = tap // 8
                                conv_store(2 * i - 4 + k, i * ROWS - 7 + 2 * k, 2, 2 * k, 2 * i - 4 + k)
                            if not last:
                                if tap == 5:
                                    normalise(n + 1, ddf)
                                if tap == 6:
                                    take_high(n + 1)
                                if tap == 7:
                                    take_middle(n + 1, 1 - par)

                    tiles(dve, step)
                    if ddf == 0:
                        dve.wait_ge(product_ready, (base + TILES) * TAPS + PRIMED)
                        total(TILES - 1, 1)
                        leaky(TILES - 1, 1)
                        for k in range(3):
                            g = CONV_GROUPS - 4 + k
                            conv_store(g, HROWS - 7 + 2 * k, 2, 2 * (k % 2), g)
                        conv_store(CONV_GROUPS - 1, HROWS - 1, 1, 2, CONV_GROUPS - 1)
                        conv_store(CONV_GROUPS - 1, 0, 1, 3, CONV_GROUPS, wait=False)

        @block.tensor
        def _(pe):
            pe.wait_ge(bias_rows, DDFS * 2 * PARTS * HALVES)
            for d in range(DDFS):
                mm = nc.tensor.matmul(p_filt[:, d:d + 1], lhsT=brow[:, d, :], rhs=ident[0:1, 0:1], start=True, stop=True)
            mm.then_inc(bias_psum, 1)
            pe.wait_ge(weights_ready, 1)

            def filt(m, i, ddf):
                pe.wait_ge(normed_ready, m + PRIMED)
                for chunk in range(2):
                    mm = nc.tensor.matmul(flat(p_filt[:, 0:CHUNK]), lhsT=wfilt[:, ddf, chunk, :],
                                          rhs=rows(source[ddf], i * ROWS + 2 * chunk + 1, 2, 1),
                                          start=(chunk == 0), stop=(chunk == 1))
                mm.then_inc(filt_ready, 1)

            def variance(m):
                pe.wait_ge(squares_ready, m + 1)
                nc.tensor.matmul(p_var[:, 0:CHUNK], lhsT=wvar[:], rhs=squares[:], start=True,
                                 stop=True).then_inc(var_ready, 1)

            def add(slot, chunk, start=False, stop=False):
                return nc.tensor.matmul(psum_rows(acc, 2 * chunk, 2), lhsT=ident[:],
                                        rhs=flat(prod[:, slot, chunk * CHUNK:(chunk + 1) * CHUNK]),
                                        start=start, stop=stop)

            with pe.Fori(0, IMAGES) as im:
                for ddf in range(DDFS):
                    base = im * PER_IMAGE + ddf * TILES
                    done, count = ((x_summed, im * PIECES + PIECES), (conv_stored, im * CONV_SUMS + CONV_SUMS),
                                   (tile_done, im * PER_IMAGE + 2 * TILES + PRIMED))[ddf]
                    pe.wait_ge(done, count)
                    filt(base, 0, ddf)
                    variance(base)
                    q = slice(32 * ddf, 32 * ddf + 32)
                    pe.wait_ge(pooled_ready, im * DDFS + ddf + 1)
                    nc.tensor.matmul(acc[q, 0:1], lhsT=w1[:, ddf, :], rhs=pooled[:], start=True,
                                     stop=True).then_inc(hidden_psum, 1)
                    pe.wait_ge(hidden_ready, im * DDFS + ddf + 1)
                    for tap in range(TAPS):
                        mm = nc.tensor.matmul(acc[:, 512 + tap:513 + tap], lhsT=w2[q, tap, :], rhs=hidden[q, :],
                                              start=True, stop=True)
                    mm.then_inc(cf_psum, 1)

                    def accumulate(i, par, tap, ddf=ddf, base=base):
                        slot2 = TAP2_SLOTS[par]
                        if tap == 1:
                            pe.wait_ge(tile_done, base + i + PRIMED)
                            add(slot2, 0, start=True)
                        if tap == 3:
                            add(slot2, 1, start=True)
                            add(SLOTS[1][5], 0)
                        if tap == 4:
                            add(SLOTS[1][5], 1)
                        if tap == 5:
                            add(SLOTS[1][8], 0)
                        if tap == 6:
                            add(SLOTS[1][8], 1)
                        if tap == 7:
                            pe.wait_ge(sum_step, added(im, ddf, i) + ADDS[ddf])
                            add(par, 0, stop=True)
                        if tap == 8:
                            add(par, 1, stop=True).then_inc(acc_ready, 1)

                    def convolve(group, r, count, bank, taps):
                        for tap in taps:
                            mm = nc.tensor.matmul(psum_rows(acc, bank, count), lhsT=wconv[:, tap, :],
                                                  rhs=rows(img_b, r + tap // 3, count, tap % 3),
                                                  start=(tap == 0), stop=(tap == TAPS - 1))
                        return mm

                    def step(i, pair, par, edge=False, last=False, ddf=ddf, base=base,
                             accumulate=accumulate, convolve=convolve):
                        n = base + i
                        pe.wait_ge(split_ready, n + 1)
                        for tap in range(TAPS):
                            first = edge and par == 0 and tap < 2
                            pe.wait_ge(product_ready, n * TAPS + (0 if first else tap - 1) + PRIMED)
                            for chunk in range(2):
                                mm = nc.tensor.matmul(psum_rows(spread[(par + tap) % 2], 2 * chunk, 2),
                                                      lhsT=wcopy[:, chunk * TAPS + tap, :],
                                                      rhs=flat(filters[:, par, :]), start=True, stop=True)
                            mm.then_inc(spread_ready, 1)
                            if tap == 0 and not last:
                                filt(n + 1, i + 1, ddf)
                            if tap == 2 and not last:
                                variance(n + 1)
                            if ddf and not (edge and par == 0):
                                accumulate(i - 1, 1 - par, tap)
                            if ddf == 0 and not edge and tap < 8:
                                if tap == 0:
                                    pe.wait_ge(tile_done, n - 1 + PRIMED)
                                lo, hi = (0, 3, 5, 7, 9, 12, 14, 16)[tap], (3, 5, 7, 9, 12, 14, 16, 18)[tap]
                                for k in range(2):
                                    taps = [t - TAPS * k for t in range(lo, hi) if t // TAPS == k]
                                    if not taps:
                                        continue
                                    if k == 1 and taps[0] == 0:
                                        pe.wait_ge(tile_done, n + PRIMED)
                                    mm = convolve(0, i * ROWS - 7 + 2 * k, 2, 2 * k, taps)
                                    if taps[-1] == TAPS - 1:
                                        mm.then_inc(conv_ready, 1)

                    tiles(pe, step)
                    if ddf:
                        pe.wait_ge(product_ready, (base + TILES) * TAPS + PRIMED)
                        for tap in range(TAPS):
                            accumulate(TILES - 1, 1, tap)
                    else:
                        every = range(TAPS)
                        for k in range(3):
                            if k == 1:
                                pe.wait_ge(tile_done, base + TILES + PRIMED)
                            pe.wait_ge(conv_stored, im * CONV_SUMS + CONV_GROUPS - 4 + k - 1)
                            convolve(0, HROWS - 7 + 2 * k, 2, 2 * (k % 2), every).then_inc(conv_ready, 1)
                        pe.wait_ge(conv_stored, im * CONV_SUMS + CONV_GROUPS - 2)
                        pe.wait_ge(halo_b, im * 64 + 32)
                        convolve(0, HROWS - 1, 1, 2, every)
                        convolve(0, 0, 1, 3, every).then_inc(conv_ready, 1)


def kernel(x, L0_conv_Ws, L0_conv_bs, L0_conv_W1, L0_conv_b1, L0_conv_W2, L0_conv_b2, L0_conv_std_ch,
           L0_conv_Wc, L0_conv_bc, L1_conv_sw1, L1_conv_sb1, L1_conv_sstd1, L1_conv_cw1_1, L1_conv_cb1_1,
           L1_conv_cw2_1, L1_conv_cb2_1, L1_conv_cstd1, L1_conv_sw2, L1_conv_sb2, L1_conv_sstd2,
           L1_conv_cw1_2, L1_conv_cb1_2, L1_conv_cw2_2, L1_conv_cb2_2, L1_conv_cstd2):
    import concourse.bacc as bacc
    from concourse.bass_utils import run_bass_kernel_spmd

    f32 = np.float32
    a = np.asarray
    wspatial = np.zeros((P, DDFS, TAPS), f32)
    bspatial = np.zeros((1, DDFS, TAPS), f32)
    w1 = np.zeros((P, DDFS, 32), f32)
    b1 = np.zeros((32 * DDFS, 1), f32)
    w2 = np.zeros((32 * DDFS, TAPS, P), f32)
    tabs = np.zeros((P, 3, DDFS, TAPS), f32)
    tabs[:, 2, 0, :] = STD_SPATIAL
    for d, (ws, bs, u1, c1, u2, c2, std) in enumerate((
            (L0_conv_Ws, L0_conv_bs, L0_conv_W1, L0_conv_b1, L0_conv_W2, L0_conv_b2, L0_conv_std_ch),
            (L1_conv_sw1, L1_conv_sb1, L1_conv_cw1_1, L1_conv_cb1_1, L1_conv_cw2_1, L1_conv_cb2_1, L1_conv_cstd1),
            (L1_conv_sw2, L1_conv_sb2, L1_conv_cw1_2, L1_conv_cb1_2, L1_conv_cw2_2, L1_conv_cb2_2, L1_conv_cstd2))):
        bspatial[0, d] = a(bs)
        b1[32 * d:32 * d + MID, 0] = a(c1)
        for half in range(HALVES):
            h = slice(half * C, (half + 1) * C)
            wspatial[h, d] = a(ws).T
            w1[h, d, :MID] = a(u1).T
            w2[32 * d:32 * d + MID, :, h] = a(u2).reshape(C, TAPS, MID).transpose(2, 1, 0)
            tabs[h, 0, d] = a(c2).reshape(C, TAPS)
            tabs[h, 1, d] = a(std).reshape(C, TAPS)
    tabs[:, 2, 1, :] = a(L1_conv_sstd1)
    tabs[:, 2, 2, :] = a(L1_conv_sstd2)
    wconv = np.zeros((P, TAPS, P), f32)
    bconv = np.zeros((P, 1), f32)
    for half in range(HALVES):
        h = slice(half * C, (half + 1) * C)
        wconv[h, :, h] = a(L0_conv_Wc).transpose(1, 2, 3, 0).reshape(C, TAPS, C)
        bconv[h, 0] = a(L0_conv_bc)
    ident = np.eye(P, dtype=f32)
    wvar = np.zeros((P, P), f32)
    for chunk in range(2):
        for r in range(FILTERS, P // 2):
            wvar[chunk * 64 + r, chunk * 64 + r] = 1.0
    wcopy = np.zeros((P, 2 * TAPS, P), f32)
    masks = np.zeros((P, 4), f32)
    masks[:, 2] = EPS
    masks[:, 3] = TINY
    for chunk in range(2):
        for part in range(PARTS):
            masks[chunk * 64 + part * 18:chunk * 64 + part * 18 + 18, 0] = -1.0 if part > 0 else 0.0
            masks[chunk * 64 + part * 18:chunk * 64 + part * 18 + 18, 1] = -1.0 if part > 1 else 0.0
            for half in range(HALVES):
                r = chunk * 64 + part * 18 + half * TAPS
                wvar[r:r + TAPS, r:r + TAPS] = 1.0 / (TAPS - 1)
                for tap in range(TAPS):
                    wcopy[r + tap, chunk * TAPS + tap, half * C:(half + 1) * C] = 1.0
    wcopy = wcopy.reshape(P, 2 * TAPS * P)

    arrays = {"x": np.ascontiguousarray(a(x)), "wspatial": wspatial, "bspatial": bspatial, "w1": w1, "b1": b1,
              "w2": w2, "tabs": tabs, "wconv": wconv, "bconv": bconv, "ident": ident, "wvar": wvar,
              "wcopy": wcopy, "masks": masks}
    nc = bacc.Bacc("TRN2", target_bir_lowering=False, num_devices=1)
    args = [nc.dram_tensor(f"in_{k}", v.shape, mybir.dt.from_np(v.dtype), kind="ExternalInput").ap()
            for k, v in arrays.items()]
    res = nc.dram_tensor("result_dram", (IMAGES, C, H, W), F32, kind="ExternalOutput").ap()
    ddf_stack_kernel(nc, *args, res)
    r = run_bass_kernel_spmd(nc, [{f"in_{k}": v for k, v in arrays.items()}], core_ids=[0])
    return r.results[0]["result_dram"]
```

```python
from contextlib import ExitStack

import numpy as np

import concourse.bass as bass
from concourse import mybir

F32 = mybir.dt.float32
BF16 = mybir.dt.bfloat16
ALU = mybir.AluOpType
ACT = mybir.ActivationFunctionType
AX_X = mybir.AxisListType.X
ds = bass.ds

IMAGES, C, H, W = 16, 64, 192, 192
TAPS, MID = 9, 12
P = 128
HALVES = 2
HROWS = H // HALVES
PITCH = W + 1
IMG = (HROWS + 2) * PITCH + 2
ROWS = 4
TILE = ROWS * W
TILES = HROWS // ROWS
CHUNK = TILE // 2
PPITCH = 256
PARTS = 3
FILTERS = PARTS * HALVES * TAPS
DDFS = 3
PER_IMAGE = DDFS * TILES
PIECE = 2 * ROWS
PIECES = HROWS // PIECE
QUARTERS = 4
BORDERS = 4
SLOPE = 0.1
EPS = 1e-10
TINY = 2.0 ** -63
STD_SPATIAL = 1.4142135623730951 / 3

CF_STEPS = 5
PRIMED = 2

RESIDUAL = "residual"
ADDED = ((1, 2, 3, 4, 5, 6, 7), (1, 3, 4, 6, 7), (RESIDUAL, 1, 3, 4, 6, 7))
SLOTS = ({1: 2, 2: 3, 3: 4, 4: 5, 5: 6, 6: 7, 7: 8}, {1: 2, 3: 3, 4: 4, 6: 2, 7: 3, 5: 7, 8: 8})
TAP2_SLOTS = (5, 6)
ADDS = tuple(len(a) for a in ADDED)
SHARED = TILES - 2
PAIRS = H // 2
HPAIRS = PAIRS // 2
BLOCKS = 6
CONV_GROUPS = TILES
STORES = CONV_GROUPS + 1
HOME = STORES * 2 * 16
MEAN_PARTS = PIECES + 2 * CONV_GROUPS + 1


def ddf_stack_kernel(nc, x, wspatial_in, bspatial_in, w1_in, b1_in, w2_in, tabs_in, wconv_in, bconv_in,
                     ident_in, wvar_in, wcopy_in, masks_in, out):
    ctx = ExitStack()
    with ctx:
        def sb(name, shape, dt=F32):
            return ctx.enter_context(nc.sbuf_tensor(name, shape, dt))

        def pb(name, shape):
            return ctx.enter_context(nc.psum_tensor(name, shape, F32))

        def sem(name):
            return ctx.enter_context(nc.semaphore(name))

        img_a = sb("img_a", [P, IMG])
        img_b = sb("img_b", [P, IMG])
        prod = sb("prod", [P, 9, TILE])
        wcopy_f32 = prod[:, 0:2, :].rearrange("p a n -> p (a n)")[:, 0:TAPS * P]
        result = sb("result", [P, 2, TILE])
        conv_pairs = sb("conv_pairs", [P, HALVES, CHUNK])
        conv_rows = sb("conv_rows", [P, TILE])
        squares = sb("squares", [P, CHUNK])
        rstd = sb("rstd", [P, CHUNK])
        normed = sb("normed", [P, CHUNK])
        high = sb("high", [P, CHUNK], BF16)
        rest = squares
        middle = sb("middle", [P, CHUNK], BF16)
        filters = sb("filters", [P, 2, CHUNK], BF16)
        wfilt = sb("wfilt", [P, DDFS, 2, P])
        wvar = sb("wvar", [P, P])
        ident = sb("ident", [P, P])
        wcopy = sb("wcopy", [P, TAPS, P], BF16)
        wconv = sb("wconv", [P, BLOCKS, P])
        bconv = sb("bconv", [P, 1])
        w1 = sb("w1", [P, DDFS, 32])
        b1 = sb("b1", [32 * DDFS, 1])
        w2 = sb("w2", [32 * DDFS, TAPS, C])
        tabs = sb("tabs", [P, 3, DDFS, TAPS])
        masks = sb("masks", [P, 4])
        wspatial = sb("wspatial", [P, DDFS, TAPS])
        wmean = sb("wmean", [P, DDFS])
        bspatial = sb("bspatial", [1, DDFS, TAPS])
        bmean = sb("bmean", [1, DDFS])
        brow = prod[0:1, 8, 0:DDFS * P].rearrange("p (d m) -> p d m", d=DDFS)
        bcol = sb("bcol", [P, DDFS])
        sums = sb("sums", [P, TILES])
        mean_parts = sb("mean_parts", [P, MEAN_PARTS])
        x_sums = mean_parts[:, 0:PIECES]
        pooled = sb("pooled", [P, 1])
        hidden = sb("hidden", [32 * DDFS, 1])
        cf_raw = sb("cf_raw", [P, TAPS])
        w2_mean = prod[0:32 * DDFS, 7, 0:C]
        b2_mean = sb("b2_mean", [P, DDFS])
        cf_sq = sb("cf_sq", [P, TAPS])
        cf_var = sb("cf_var", [P, 1])
        cf_std = sb("cf_std", [P, 1])
        cf_inv = sb("cf_inv", [P, 1])
        cf = sb("cf", [P, TAPS])

        spread = [pb(f"spread{i}", [P, ROWS * PPITCH]) for i in range(2)]
        acc = pb("acc", [P, ROWS * PPITCH])
        p_filt = pb("p_filt", [P, 512])
        p_var = pb("p_var", [P, 512])
        p_hidden = spread[1][:, 0:1]
        p_cf = spread[1][:, 2 * PPITCH:2 * PPITCH + TAPS]

        consts_in = sem("consts_in")
        zeroed = sem("zeroed")
        prep = sem("prep")
        channel_prep = sem("channel_prep")
        bias_rows = sem("bias_rows")
        bias_psum = sem("bias_psum")
        weights_ready = sem("weights_ready")
        x_first = [sem(f"x_first{i}") for i in range(QUARTERS)]
        x_in = sem("x_in")
        x_summed = sem("x_summed")
        edge_zeroed = sem("edge_zeroed")
        paired = [sem(f"paired{i}") for i in range(2)]
        halo_a = sem("halo_a")
        halo_b = sem("halo_b")
        filt_ready = sem("filt_ready")
        squares_ready = sem("squares_ready")
        var_ready = sem("var_ready")
        inv_step = sem("inv_step")
        normed_ready = sem("normed_ready")
        high_ready = sem("high_ready")
        rest_ready = sem("rest_ready")
        middle_ready = sem("middle_ready")
        split_ready = sem("split_ready")
        spread_ready = sem("spread_ready")
        product_ready = sem("product_ready")
        sum_step = sem("sum_step")
        acc_ready = sem("acc_ready")
        residual_added = sem("residual_added")
        row_added = sem("row_added")
        total_ready = sem("total_ready")
        tile_done = sem("tile_done")
        conv_ready = sem("conv_ready")
        conv_staged = sem("conv_staged")
        conv_home = [sem(f"conv_home{i}") for i in range(2)]
        conv_stored = sem("conv_stored")
        pooled_ready = sem("pooled_ready")
        hidden_psum = sem("hidden_psum")
        hidden_ready = sem("hidden_ready")
        cf_psum = sem("cf_psum")
        cf_step = sem("cf_step")
        cf_std_step = sem("cf_std_step")
        stored = [sem(f"stored{i}") for i in range(2)]

        def added(im, ddf, i=0):
            return im * (TILES * sum(ADDS)) + (TILES * sum(ADDS[:ddf]) + PRIMED) + i * ADDS[ddf]

        def rows(img, r, count, dv):
            return img[:, ds(r * PITCH + dv, count * PITCH)].rearrange("p (r w) -> p r w", w=PITCH)[:, :, 0:W]

        def psum_rows(t, r=0, count=ROWS):
            return t[:, r * PPITCH:(r + count) * PPITCH].rearrange("p (r w) -> p r w", w=PPITCH)[:, :, 0:W]

        def flat(t):
            return t.rearrange("p (r w) -> p r w", w=W)

        def zero_borders(eng, img):
            last = (HROWS + 1) * PITCH
            for part in (img[:, 0:last + PITCH].rearrange("p (r w) -> p r w", w=PITCH)[:, :, 0:1],
                         img[:, last + PITCH:IMG], img[:, 1:PITCH], img[:, last + 1:last + PITCH]):
                eng.memset(part, 0.0).then_inc(zeroed, 1)

        def half_groups(k):
            return 2 * ({0: CONV_GROUPS - 2, CONV_GROUPS - 1: CONV_GROUPS - 1}.get(k, k - 1) if isinstance(k, int)
                        else k - 1)

        def stores(k):
            return {0: CONV_GROUPS - 2, CONV_GROUPS - 1: STORES - 1}.get(k, k - 1) if isinstance(k, int) else k - 1

        def following(ddf, more):
            return (None, 2, 0 if more else None)[ddf]

        def started(i, first):
            return not isinstance(i, int) or i >= first

        def tiles(eng, step, peeled=2, opened=False):
            if not opened:
                step(0, 0, 0, edge=True)
            step(1, 0, 1, edge=True)
            if peeled == 4:
                step(2, 1, 0)
                step(3, 1, 1)
            with eng.Fori(peeled // 2, TILES // 2 - 1) as pair:
                step(2 * pair, pair, 0)
                step(2 * pair + 1, pair, 1)
            step(TILES - 2, TILES // 2 - 1, 0)
            step(TILES - 1, TILES // 2 - 1, 1, last=True)

        source = (img_a, img_a, img_b)

        block = ctx.enter_context(nc.Block())

        @block.sync
        def _(sp):
            for primed in (normed_ready, product_ready, sum_step, tile_done, conv_staged, conv_stored, residual_added,
                           x_in, *stored, *paired, *conv_home):
                sp.sem_inc(primed, PRIMED)
            for dst, src in ((wspatial[:], wspatial_in), (bspatial[:], bspatial_in), (w1[:], w1_in), (b1[:], b1_in),
                             (w2[:], w2_in), (tabs[:], tabs_in), (wconv[:], wconv_in), (bconv[:], bconv_in),
                             (ident[:], ident_in), (wvar[:], wvar_in), (wcopy_f32, wcopy_in), (masks[:], masks_in)):
                sp.dma_start(dst, src).then_inc(consts_in, 16)

            def load(image, start, count, signal):
                for half in range(HALVES):
                    above = 1 if isinstance(start, int) and start == 0 and half == 1 else 0
                    below = 1 if isinstance(start, int) and start + count == HROWS and half == 0 else 0
                    n = count + above + below
                    dst = img_a[half * C:(half + 1) * C, ds((start + 1 - above) * PITCH + 1, n * PITCH)]
                    sp.dma_start(dst.rearrange("p (r w) -> p r w", w=PITCH)[:, :, 0:W],
                                 x[ds(image, 1), :, ds(half * HROWS + start - above, n), :]
                                 .rearrange("b c r w -> (b c) r w")).then_inc(signal, 16)

            def image_body(im, more):
                base = im * PER_IMAGE

                def pair_rows(i, par):
                    sp.wait_ge(tile_done, base + i + 1 + PRIMED)
                    for half in range(HALVES):
                        tile = flat(result[half * C:(half + 1) * C, par, :])
                        for low in range(2):
                            slot = 2 * i + half * HPAIRS + low
                            dst = img_b[(1 - low) * C:(2 - low) * C, ds(slot * PITCH + 1, 2 * PITCH)]
                            sp.dma_start(dst.rearrange("p (r w) -> p r w", w=PITCH)[:, :, 0:W],
                                         tile[:, low::2, :]).then_inc(paired[par], 16)

                def unpair(k, half):
                    sp.wait_ge(conv_staged, im * (2 * CONV_GROUPS) + half_groups(k) + half + 1 + PRIMED)
                    for odd in range(2):
                        dst = flat(conv_rows[half * C:(half + 1) * C, :])[:, odd::2, :]
                        sp.dma_start(dst, flat(conv_pairs[odd * C:(odd + 1) * C, half, :]))\
                          .then_inc(conv_home[half], 16)

                def unpair_group_0():
                    for part in range(2):
                        sp.wait_ge(conv_staged, im * (2 * CONV_GROUPS) + half_groups(0) + part + 1 + PRIMED)
                        for half in range(HALVES):
                            for odd in range(2):
                                row = (2 if part == half else 0) + odd
                                sp.dma_start(conv_rows[half * C:(half + 1) * C, row * W:(row + 1) * W],
                                             conv_pairs[odd * C:(odd + 1) * C, part, half * W:(half + 1) * W])\
                                  .then_inc(conv_home[part], 16)

                def ddf1_step(i, pair, par, edge=False, last=False):
                    if started(i, 1):
                        pair_rows(i - 1, 1 - par)
                    if started(i, 3):
                        unpair(i - 2, 0)
                        unpair(i - 2, 1)

                tiles(sp, ddf1_step, 4)
                pair_rows(TILES - 1, 1)
                unpair(CONV_GROUPS - 2, 0)
                unpair(CONV_GROUPS - 2, 1)
                unpair_group_0()

                for img, done, count, signal in (
                        (img_a, conv_stored, im * STORES + stores(CONV_GROUPS - 1) + PRIMED, halo_a),
                        (img_b, tile_done, base + 2 * TILES + PRIMED, halo_b)):
                    sp.wait_ge(done, count)
                    sp.dma_start(img[0:C, (HROWS + 1) * PITCH + 1:(HROWS + 1) * PITCH + 1 + W],
                                 img[C:P, PITCH + 1:PITCH + 1 + W]).then_inc(signal, 16)
                    sp.dma_start(img[C:P, 1:1 + W],
                                 img[0:C, HROWS * PITCH + 1:HROWS * PITCH + 1 + W]).then_inc(signal, 16)
                    if img is img_a:
                        unpair(CONV_GROUPS - 1, 0)
                        unpair(CONV_GROUPS - 1, 1)

                def store(i, par):
                    sp.wait_ge(tile_done, base + 2 * TILES + i + 1 + PRIMED)
                    for half in range(HALVES):
                        dst = out[ds(im, 1), :, ds(i * ROWS + half * HROWS, ROWS), :]
                        sp.dma_start(dst.rearrange("b c r w -> (b c) (r w)"),
                                     result[half * C:(half + 1) * C, par, :]).then_inc(stored[par], 16)

                def turn(piece):
                    if started(piece, 1):
                        store(2 * piece - 2, 0)
                        store(2 * piece - 1, 1)
                    if more:
                        sp.wait_ge(sum_step, added(im, 2, 2 * piece + 1) + 1)
                        if not isinstance(piece, int) or piece < SHARED // 2:
                            sp.wait_ge(residual_added, im * SHARED + 2 * piece + 2 + PRIMED)
                        sp.wait_ge(x_in, (im * PIECES + piece) * (HALVES * 16) + PRIMED)
                        load(im + 1, piece * PIECE, PIECE, x_in)

                turn(0)
                with sp.Fori(1, PIECES - 1) as piece:
                    turn(piece)
                turn(PIECES - 1)
                store(TILES - 2, 0)
                store(TILES - 1, 1)

            sp.wait_ge(zeroed, 2 * BORDERS)
            for quarter in range(QUARTERS):
                load(0, quarter * HROWS // QUARTERS, HROWS // QUARTERS, x_first[quarter])
            with sp.Fori(0, IMAGES - 1) as im:
                image_body(im, True)
            image_body(IMAGES - 1, False)
            for par in range(2):
                sp.wait_ge(stored[par], IMAGES * TILES // 2 * HALVES * 16 + PRIMED)

        @block.gpsimd
        def _(pool):
            zero_borders(nc.gpsimd, img_a)
            pool.wait_ge(weights_ready, 1)

            with pool.Fori(0, IMAGES) as im:
                for ddf in range(DDFS):
                    base = im * PER_IMAGE + ddf * TILES

                    def step(i, par, last=False, ddf=ddf, base=base):
                        total = prod[:, par, :]
                        for k, tap in enumerate(ADDED[ddf]):
                            if tap == RESIDUAL:
                                pool.wait_ge(product_ready, (base + i) * TAPS + 1 + PRIMED)
                                count = ROWS if last else ROWS // 2
                                nc.gpsimd.tensor_tensor(out=flat(total[:, 0:count * W]),
                                                        in0=flat(total[:, 0:count * W]),
                                                        in1=rows(img_a, i * ROWS + 1, count, 1),
                                                        op=ALU.add).then_inc(sum_step, 1)
                                continue
                            pool.wait_ge(product_ready, (base + i) * TAPS + tap + 1 + PRIMED)
                            if k:
                                pool.wait_ge(sum_step, added(im, ddf, i) + k)
                            nc.gpsimd.tensor_tensor(out=total, in0=total, in1=prod[:, SLOTS[ddf > 0][tap], :],
                                                    op=ALU.add).then_inc(sum_step, 1)

                    with pool.Fori(0, SHARED // 2) as pair:
                        step(2 * pair, 0)
                        step(2 * pair + 1, 1)
                    step(SHARED, 0, last=True)
                    step(SHARED + 1, 1, last=True)

        @block.scalar
        def _(act):
            nc.scalar.preload_act_table_set("natural_log_exp_and_others")
            act.wait_ge(weights_ready, 1)

            def invert(m, ddf):
                act.wait_ge(filt_ready, m + 1)
                nc.scalar.activation(squares[:], p_filt[:, 0:CHUNK], ACT.Square,
                                     bias=bcol[:, ddf:ddf + 1]).then_inc(squares_ready, 1)
                act.wait_ge(var_ready, m + 1)
                act.wait_ge(normed_ready, m + PRIMED)
                nc.scalar.activation(rstd[:], p_var[:, 0:CHUNK], ACT.Ln, bias=masks[:, 3:4]).then_inc(inv_step, 1)
                act.wait_ge(inv_step, 4 * m + 1)
                nc.scalar.activation(rstd[:], rstd[:], ACT.Exp, scale=0.5).then_inc(inv_step, 1)
                act.wait_ge(inv_step, 4 * m + 2)
                nc.scalar.activation(rstd[:], rstd[:], ACT.Ln, bias=masks[:, 2:3]).then_inc(inv_step, 1)
                act.wait_ge(inv_step, 4 * m + 3)
                nc.scalar.activation(rstd[:], rstd[:], ACT.Exp, scale=-1.0).then_inc(inv_step, 1)

            def round_parts(m):
                act.wait_ge(normed_ready, m + 1 + PRIMED)
                nc.scalar.activation(high[:], normed[:], ACT.Copy).then_inc(high_ready, 1)
                act.wait_ge(rest_ready, m + 1)
                nc.scalar.activation(middle[:], rest[:], ACT.Copy).then_inc(middle_ready, 1)

            def sum_x(piece):
                v = img_a[:, ds((piece * PIECE + 1) * PITCH + 1, PIECE * PITCH)]
                nc.scalar.activation(v, v, ACT.Copy, accum_out=x_sums[:, ds(piece, 1)]).then_inc(x_summed, 1)

            def channel_filters(im, ddf, meanwhile=lambda: None):
                q = slice(32 * ddf, 32 * ddf + 32)
                act.wait_ge(hidden_psum, im * DDFS + ddf + 1)
                nc.scalar.activation(hidden[q, :], p_hidden[q, :], ACT.Relu, bias=b1[q, :],
                                     scale=1.0 / (H * W)).then_inc(hidden_ready, 1)
                meanwhile()
                act.wait_ge(cf_step, (im * DDFS + ddf) * CF_STEPS + 2)
                nc.scalar.activation(cf_std[:], cf_var[:], ACT.Ln, bias=masks[:, 3:4],
                                     scale=1.0 / (TAPS - 1)).then_inc(cf_std_step, 1)
                act.wait_ge(cf_std_step, (im * DDFS + ddf) * 2 + 1)
                nc.scalar.activation(cf_std[:], cf_std[:], ACT.Exp, scale=0.5).then_inc(cf_std_step, 1)

            def stage(im, k, half):
                q = half_groups(k) + half
                act.wait_ge(conv_ready, im * (2 * CONV_GROUPS) + q + 1)
                if half == 0:
                    act.wait_ge(conv_stored, im * STORES + stores(k) + PRIMED)
                nc.scalar.activation(flat(conv_pairs[:, half, :]), psum_rows(acc, 2 * half, 2), ACT.Copy,
                                     accum_out=mean_parts[:, ds(PIECES + q, 1)]).then_inc(conv_staged, 1)

            def open_image(im, meanwhile=lambda: None):
                channel_filters(im, 0)
                invert(im * PER_IMAGE + 1, 0)
                meanwhile()
                round_parts(im * PER_IMAGE + 1)

            def image_body(im, more):
                for ddf in range(DDFS):
                    base = im * PER_IMAGE + ddf * TILES
                    if ddf == 1:
                        invert(base, ddf)
                        stage(im, CONV_GROUPS - 1, 1)
                        channel_filters(im, ddf, lambda base=base: round_parts(base))
                    if ddf == 2:
                        channel_filters(im, ddf)

                    def finish(i, pair, par, ddf=ddf, base=base):
                        if ddf == 2:
                            act.wait_ge(stored[par], (im * (TILES // 2) + pair) * (HALVES * 16) + PRIMED)
                        act.wait_ge(acc_ready, im * (2 * TILES) + (ddf - 1) * TILES + i + 1)
                        if ddf == 1:
                            nc.scalar.activation(rows(img_b, i * ROWS + 1, ROWS, 1), psum_rows(acc), ACT.Relu,
                                                 accum_out=sums[:, ds(i, 1)]).then_inc(tile_done, 1)
                        else:
                            nc.scalar.activation(flat(result[:, par, :]), psum_rows(acc),
                                                 ACT.Copy).then_inc(tile_done, 1)

                    def step(i, pair, par, edge=False, last=False, ddf=ddf, base=base, finish=finish):
                        if ddf and not edge:
                            finish(i - 2, pair - 1, par)
                        follows = following(ddf, more) if last else ddf
                        if follows is not None:
                            invert(base + i + 1, follows)
                        if ddf == 0 and started(i, 3):
                            stage(im, i - 2, 0)
                        if follows is not None:
                            round_parts(base + i + 1)
                        if ddf == 2 and more and par == 1 and started(i, 3):
                            act.wait_ge(x_in, (im * PIECES + pair) * (HALVES * 16) + PRIMED)
                            sum_x(pair - 1)
                        if ddf == 0 and started(i, 3):
                            stage(im, i - 2, 1)
                        if ddf == 2 and more and last:
                            act.wait_ge(x_in, (im + 1) * (PIECES * HALVES * 16) + PRIMED)
                            sum_x(PIECES - 1)

                    tiles(act, step, 2 if ddf else 4, opened=(ddf == 0))
                    if ddf == 0:
                        for k in (CONV_GROUPS - 2, 0):
                            for half in range(HALVES):
                                stage(im, k, half)
                        stage(im, CONV_GROUPS - 1, 0)
                    else:
                        finish(TILES - 2, TILES // 2 - 1, 0)
                        if ddf == 2 and more:
                            open_image(im + 1, lambda finish=finish: finish(TILES - 1, TILES // 2 - 1, 1))
                        else:
                            finish(TILES - 1, TILES // 2 - 1, 1)

            for piece in range(PIECES):
                if piece % (PIECES // QUARTERS) == 0:
                    act.wait_ge(x_first[piece * QUARTERS // PIECES], HALVES * 16)
                sum_x(piece)
            invert(0, 0)
            round_parts(0)
            open_image(0)
            with act.Fori(0, IMAGES - 1) as im:
                image_body(im, True)
            image_body(IMAGES - 1, False)

        @block.vector
        def _(dve):
            zero_borders(nc.vector, img_b)
            nc.vector.memset(wfilt[:], 0.0).then_inc(prep, 1)
            nc.vector.memset(brow, 1.0).then_inc(prep, 1)
            dve.wait_ge(consts_in, 12 * 16)
            nc.vector.tensor_reduce(wmean[:], wspatial[:], AX_X, ALU.add).then_inc(prep, 1)
            nc.vector.tensor_reduce(bmean[:], bspatial[:], AX_X, ALU.add).then_inc(prep, 1)
            dve.wait_ge(prep, 4)
            nc.vector.tensor_scalar(wmean[:], wmean[:], -1.0 / TAPS, None, ALU.mult).then_inc(prep, 1)
            nc.vector.tensor_scalar(bmean[:], bmean[:], -1.0 / TAPS, None, ALU.mult).then_inc(prep, 1)
            dve.wait_ge(prep, 6)
            for d in range(DDFS):
                nc.vector.tensor_scalar(wspatial[:, d, :], wspatial[:, d, :], wmean[:, d:d + 1], None,
                                        ALU.add).then_inc(prep, 1)
                nc.vector.tensor_scalar(bspatial[:, d, :], bspatial[:, d, :], bmean[:, d:d + 1], None,
                                        ALU.add).then_inc(prep, 1)
            dve.wait_ge(prep, 6 + 2 * DDFS)
            for d in range(DDFS):
                for chunk in range(2):
                    for part in range(PARTS):
                        for half in range(HALVES):
                            at = (part * HALVES + half) * TAPS
                            h = slice(half * C, (half + 1) * C)
                            nc.vector.tensor_copy(wfilt[h, d, chunk, chunk * 64 + at:chunk * 64 + at + TAPS],
                                                  wspatial[h, d, :]).then_inc(prep, 1)
                            nc.vector.tensor_copy(brow[:, d, chunk * 64 + at:chunk * 64 + at + TAPS],
                                                  bspatial[:, d, :]).then_inc(bias_rows, 1)
            nc.vector.tensor_copy(wcopy[:].rearrange("p a n -> p (a n)"), wcopy_f32).then_inc(prep, 1)
            nc.vector.tensor_tensor(out=tabs[:, 1], in0=tabs[:, 1], in1=tabs[:, 2], op=ALU.mult).then_inc(prep, 1)
            dve.wait_ge(bias_psum, 1)
            nc.vector.tensor_copy(bcol[:], p_filt[:, 0:DDFS]).then_inc(prep, 1)
            nc.vector.tensor_reduce(w2_mean, w2[:].rearrange("q t c -> q c t"), AX_X, ALU.add).then_inc(channel_prep, 1)
            nc.vector.tensor_reduce(b2_mean[:], tabs[:, 0], AX_X, ALU.add).then_inc(channel_prep, 1)
            dve.wait_ge(channel_prep, 2)
            nc.vector.tensor_scalar(w2_mean, w2_mean, -1.0 / TAPS, None, ALU.mult).then_inc(channel_prep, 1)
            nc.vector.tensor_scalar(b2_mean[:], b2_mean[:], -1.0 / TAPS, None, ALU.mult).then_inc(channel_prep, 1)
            dve.wait_ge(channel_prep, 4)
            for tap in range(TAPS):
                nc.vector.tensor_tensor(out=w2[:, tap, :], in0=w2[:, tap, :], in1=w2_mean,
                                        op=ALU.add).then_inc(channel_prep, 1)
            for d in range(DDFS):
                nc.vector.tensor_scalar(tabs[:, 0, d, :], tabs[:, 0, d, :], b2_mean[:, d:d + 1], None,
                                        ALU.add).then_inc(channel_prep, 1)
            dve.wait_ge(channel_prep, 4 + TAPS + DDFS)
            nc.vector.tensor_scalar(mean_parts[:, MEAN_PARTS - 1:], bconv[:], float(H * W // 2), None,
                                    ALU.mult).then_inc(prep, 1)
            dve.wait_ge(prep, 6 + 2 * DDFS + DDFS * 2 * PARTS * HALVES + 4)
            nc.vector.memset(sums[:], 0.0).then_inc(weights_ready, 1)
            dve.wait_ge(weights_ready, 1)

            def normalise(m, ddf):
                dve.wait_ge(inv_step, 4 * m + 4)
                nc.vector.scalar_tensor_tensor(out=normed[:], in0=p_filt[:, 0:CHUNK], scalar=bcol[:, ddf:ddf + 1],
                                               in1=rstd[:], op0=ALU.add, op1=ALU.mult).then_inc(normed_ready, 1)

            def take_high(m):
                dve.wait_ge(high_ready, m + 1)
                nc.vector.scalar_tensor_tensor(out=rest[:], in0=high[:], scalar=masks[:, 0:1], in1=normed[:],
                                               op0=ALU.mult, op1=ALU.add).then_inc(rest_ready, 1)

            def take_middle(m, par):
                dve.wait_ge(middle_ready, m + 1)
                nc.vector.scalar_tensor_tensor(out=filters[:, par, :], in0=middle[:], scalar=masks[:, 1:2],
                                               in1=rest[:], op0=ALU.mult, op1=ALU.add).then_inc(split_ready, 1)

            def mean(im, ddf):
                done, count = ((x_summed, im * PIECES + PIECES),
                               (conv_staged, (im + 1) * (2 * CONV_GROUPS) + PRIMED),
                               (tile_done, im * PER_IMAGE + 2 * TILES + PRIMED))[ddf]
                dve.wait_ge(done, count)
                nc.vector.tensor_reduce(pooled[:], (x_sums, mean_parts[:], sums[:])[ddf],
                                        AX_X, ALU.add).then_inc(pooled_ready, 1)

            def channel_filters(im, ddf):
                at = (im * DDFS + ddf) * CF_STEPS
                dve.wait_ge(cf_psum, im * DDFS + ddf + 1)
                nc.vector.tensor_tensor(out=cf_raw[:], in0=p_cf, in1=tabs[:, 0, ddf, :],
                                        op=ALU.add).then_inc(cf_step, 1)
                dve.wait_ge(cf_step, at + 1)
                nc.vector.scalar_tensor_tensor(out=cf_sq[:], in0=cf_raw[:], scalar=1.0, in1=cf_raw[:], op0=ALU.mult,
                                               op1=ALU.mult, accum_out=cf_var[:]).then_inc(cf_step, 1)
                dve.wait_ge(cf_std_step, (im * DDFS + ddf) * 2 + 2)
                nc.vector.tensor_scalar(cf_std[:], cf_std[:], EPS, None, ALU.add).then_inc(cf_step, 1)
                dve.wait_ge(cf_step, at + 3)
                nc.vector.reciprocal(cf_inv[:], cf_std[:]).then_inc(cf_step, 1)
                dve.wait_ge(cf_step, at + 4)
                nc.vector.scalar_tensor_tensor(out=cf[:], in0=cf_raw[:], scalar=cf_inv[:, 0:1],
                                               in1=tabs[:, 1, ddf, :], op0=ALU.mult,
                                               op1=ALU.mult).then_inc(cf_step, 1)
                dve.wait_ge(cf_step, at + 5)

            def image_body(im, more):

                def total(i, par):
                    dve.wait_ge(sum_step, added(im, 0, i) + ADDS[0])
                    nc.vector.tensor_tensor(out=result[:, par, :], in0=prod[:, par, :], in1=result[:, par, :],
                                            op=ALU.add).then_inc(total_ready, 1)

                def leaky(i, par):
                    dve.wait_ge(total_ready, im * TILES + i + 1)
                    nc.vector.scalar_tensor_tensor(out=result[:, par, :], in0=result[:, par, :],
                                                   scalar=SLOPE, in1=result[:, par, :], op0=ALU.mult,
                                                   op1=ALU.max).then_inc(tile_done, 1)

                def conv_store(k, r, at=0, count=ROWS):
                    homes = stores(k) + (2 if isinstance(k, int) and k == 0 else 1)
                    for half in range(HALVES):
                        dve.wait_ge(conv_home[half], im * HOME + homes * 32 + PRIMED)
                    nc.vector.scalar_tensor_tensor(out=rows(img_a, r + 1, count, 1),
                                                   in0=flat(conv_rows[:, at * W:(at + count) * W]),
                                                   scalar=bconv[:, 0:1], in1=rows(img_a, r + 1, count, 1),
                                                   op0=ALU.add, op1=ALU.add).then_inc(conv_stored, 1)

                for ddf in range(DDFS):
                    base = im * PER_IMAGE + ddf * TILES
                    if ddf == 0:
                        nc.vector.memset(img_b[C:P, PAIRS * PITCH + 1:PAIRS * PITCH + 1 + W], 0.0)\
                          .then_inc(edge_zeroed, 1)
                    else:
                        if ddf == 1:
                            normalise(base, ddf)
                        mean(im, ddf)
                        if ddf == 1:
                            take_high(base)
                            take_middle(base, 0)
                        channel_filters(im, ddf)
                        if ddf == 1:
                            conv_store(CONV_GROUPS - 1, 4 * (CONV_GROUPS - 1) - 2)
                        dve.wait_ge((halo_a, halo_b)[ddf - 1], im * 32 + 32)

                    def step(i, pair, par, edge=False, last=False, ddf=ddf, base=base):
                        n = base + i
                        first = edge and par == 0
                        for tap in range(TAPS):
                            if tap == 0:
                                dst = prod[:, par, :]
                            elif tap == 2 and ddf:
                                dst = prod[:, TAP2_SLOTS[par], :]
                            elif tap == 8 and ddf == 0:
                                dst = result[:, par, :]
                            else:
                                dst = prod[:, SLOTS[ddf > 0][tap], :]
                            if ddf == 0 and 1 <= tap <= 7 and not first:
                                dve.wait_ge(sum_step, added(im, ddf, i - 1) + tap)
                            if ddf == 0 and tap == 1 and first:
                                dve.wait_ge(sum_step, added(im, 0))
                            if ddf and tap in (1, 3, 4) and not first:
                                held = {1: 6, 3: 7, 4: 4}[tap]
                                dve.wait_ge(sum_step, added(im, ddf, i - 1) + ADDED[ddf].index(held) + 1)
                            if ddf and tap in (6, 7):
                                held = {6: 1, 7: 3}[tap]
                                dve.wait_ge(sum_step, added(im, ddf, i) + ADDED[ddf].index(held) + 1)
                            if ddf == 0 and tap == 8 and edge:
                                dve.wait_ge(stored[par], im * (TILES // 2 * HALVES * 16) + PRIMED)
                            if ddf == 0 and tap == 8:
                                dve.wait_ge(paired[par], (im * (TILES // 2) + pair) * (2 * HALVES * 16) + PRIMED)
                            dve.wait_ge(spread_ready, n * TAPS + tap + 1)
                            nc.vector.scalar_tensor_tensor(
                                out=flat(dst), in0=rows(source[ddf], i * ROWS + tap // 3, ROWS, tap % 3),
                                scalar=cf[:, tap:tap + 1], in1=psum_rows(spread[(par + tap) % 2]),
                                op0=ALU.mult, op1=ALU.mult).then_inc(product_ready, 1)
                            if ddf == 2 and tap == 7 and not (isinstance(i, int) and i >= SHARED):
                                dve.wait_ge(product_ready, n * TAPS + 6 + PRIMED)
                                row = prod[:, SLOTS[1][5], (ROWS - 1) * W:]
                                nc.vector.tensor_tensor(out=flat(row), in0=flat(row),
                                                        in1=rows(img_a, i * ROWS + ROWS, 1, 1),
                                                        op=ALU.add).then_inc(row_added, 1)
                            if ddf == 0 and not first:
                                if tap == 1:
                                    total(i - 1, 1 - par)
                                if tap == 2:
                                    leaky(i - 1, 1 - par)
                            if ddf == 0 and tap == 3 and started(i, 4):
                                conv_store(i - 3, 4 * (i - 3) - 2)
                            follows = following(ddf, more) if last else ddf
                            if follows is not None:
                                if tap == 4:
                                    normalise(n + 1, follows)
                                if tap == 5:
                                    take_high(n + 1)
                                if tap == 6:
                                    take_middle(n + 1, 1 - par)

                    tiles(dve, step, 2 if ddf else 4)
                    if ddf == 0:
                        dve.wait_ge(product_ready, (base + TILES) * TAPS + PRIMED)
                        total(TILES - 1, 1)
                        leaky(TILES - 1, 1)
                        for k in (CONV_GROUPS - 3, CONV_GROUPS - 2):
                            conv_store(k, 4 * k - 2)
                        conv_store(0, 0, 0, 2)
                        conv_store(0, HROWS - 2, 2, 2)
                    if ddf == 2 and more:
                        mean(im + 1, 0)
                        channel_filters(im + 1, 0)

            mean(0, 0)
            normalise(0, 0)
            take_high(0)
            take_middle(0, 0)
            channel_filters(0, 0)
            with dve.Fori(0, IMAGES - 1) as im:
                image_body(im, True)
            image_body(IMAGES - 1, False)

        @block.tensor
        def _(pe):
            pe.wait_ge(bias_rows, DDFS * 2 * PARTS * HALVES)
            for d in range(DDFS):
                mm = nc.tensor.matmul(p_filt[:, d:d + 1], lhsT=brow[:, d, :], rhs=ident[0:1, 0:1],
                                      start=True, stop=True)
            mm.then_inc(bias_psum, 1)
            pe.wait_ge(weights_ready, 1)

            def filt(m, i, ddf, chunks=range(2)):
                for chunk in chunks:
                    if chunk == 0:
                        pe.wait_ge(normed_ready, m + PRIMED)
                    mm = nc.tensor.matmul(flat(p_filt[:, 0:CHUNK]), lhsT=wfilt[:, ddf, chunk, :],
                                          rhs=rows(source[ddf], i * ROWS + 2 * chunk + 1, 2, 1),
                                          start=(chunk == 0), stop=(chunk == 1))
                    if chunk == 1:
                        mm.then_inc(filt_ready, 1)

            def variance(m):
                pe.wait_ge(squares_ready, m + 1)
                nc.tensor.matmul(p_var[:, 0:CHUNK], lhsT=wvar[:], rhs=squares[:], start=True,
                                 stop=True).then_inc(var_ready, 1)

            def add(slot, chunk, start=False, stop=False):
                return nc.tensor.matmul(psum_rows(acc, 2 * chunk, 2), lhsT=ident[:],
                                        rhs=flat(prod[:, slot, chunk * CHUNK:(chunk + 1) * CHUNK]),
                                        start=start, stop=stop)

            def spread_filter(n, par, tap, first, chain):
                first = first and tap < 2
                pe.wait_ge(product_ready, n * TAPS + (0 if first else tap - 1) + PRIMED)
                if first and tap == 1:
                    pe.wait_ge(cf_step, chain * CF_STEPS + 1)
                for chunk in range(2):
                    c = slice(chunk * P // 2, (chunk + 1) * P // 2)
                    mm = nc.tensor.matmul(psum_rows(spread[(par + tap) % 2], 2 * chunk, 2),
                                          lhsT=wcopy[c, tap, :], rhs=flat(filters[c, par, :]),
                                          start=True, stop=True)
                mm.then_inc(spread_ready, 1)

            def open_image(im, meanwhile=lambda tap: None):
                channel_filters(im, 0)
                n = im * PER_IMAGE
                pe.wait_ge(split_ready, n + 1)
                for tap in range(TAPS):
                    spread_filter(n, 0, tap, True, im * DDFS)
                    if tap < 2:
                        filt(n + 1, 1, 0, (tap,))
                    if tap == 2:
                        variance(n + 1)
                    meanwhile(tap)
                    if tap == TAPS - 1:
                        filt(n + 2, 2, 0, (0,))

            def channel_filters(im, ddf):
                q = slice(32 * ddf, 32 * ddf + 32)
                pe.wait_ge(pooled_ready, im * DDFS + ddf + 1)
                nc.tensor.matmul(p_hidden[q, :], lhsT=w1[:, ddf, :], rhs=pooled[:], start=True,
                                 stop=True).then_inc(hidden_psum, 1)
                pe.wait_ge(hidden_ready, im * DDFS + ddf + 1)
                for half in range(HALVES):
                    for tap in range(TAPS):
                        mm = nc.tensor.matmul(p_cf[half * C:(half + 1) * C, tap:tap + 1], lhsT=w2[q, tap, :],
                                              rhs=hidden[q, :], start=True, stop=True)
                mm.then_inc(cf_psum, 1)

            def convolve(slot, count, out_ap, blocks=range(BLOCKS)):
                for block in blocks:
                    mm = nc.tensor.matmul(out_ap, lhsT=wconv[:, block, :],
                                          rhs=rows(img_b, slot + block // 3, count, block % 3),
                                          start=(block == 0), stop=(block == BLOCKS - 1))
                return mm

            def image_body(im, more):

                def group(k, half, blocks=range(BLOCKS)):
                    if blocks[0] == 0:
                        pe.wait_ge(conv_staged, im * (2 * CONV_GROUPS) + half_groups(k) + half - 1 + PRIMED)
                    mm = convolve(2 * k - 1 + half * HPAIRS, 2, psum_rows(acc, 2 * half, 2), blocks)
                    if blocks[-1] == BLOCKS - 1:
                        mm.then_inc(conv_ready, 1)

                for ddf in range(DDFS):
                    base = im * PER_IMAGE + ddf * TILES
                    if ddf:
                        channel_filters(im, ddf)

                    def accumulate(i, par, tap, ddf=ddf, base=base):
                        if tap == 1:
                            pe.wait_ge(tile_done, base + i + PRIMED)
                            add(SLOTS[1][5], 0, start=True)
                        if tap == 3:
                            if ddf == 2 and not (isinstance(i, int) and i >= SHARED):
                                pe.wait_ge(row_added, im * SHARED + i + 1)
                            add(SLOTS[1][5], 1, start=True)
                        if tap == 4:
                            add(SLOTS[1][8], 0)
                            add(SLOTS[1][8], 1)
                        if tap == 5:
                            add(TAP2_SLOTS[par], 0)
                            add(TAP2_SLOTS[par], 1)
                        if tap == 6:
                            if ddf == 2 and not (isinstance(i, int) and i >= SHARED):
                                nc.tensor.matmul(psum_rows(acc, 2, 1), lhsT=ident[:],
                                                 rhs=rows(img_a, i * ROWS + 3, 1, 1), start=False,
                                                 stop=False).then_inc(residual_added, 1)
                            pe.wait_ge(sum_step, added(im, ddf, i) + ADDS[ddf])
                            add(par, 0, stop=True)
                        if tap == 7:
                            add(par, 1, stop=True).then_inc(acc_ready, 1)

                    def step(i, pair, par, edge=False, last=False, ddf=ddf, base=base,
                             accumulate=accumulate, group=group):
                        n = base + i
                        first = edge and par == 0
                        last_but_one = isinstance(i, int) and i == TILES - 2
                        pe.wait_ge(split_ready, n + 1)
                        for tap in range(TAPS):
                            spread_filter(n, par, tap, first, im * DDFS + ddf)
                            follows = following(ddf, more) if last else ddf
                            if follows is not None:
                                if tap == 0 or tap == 1 and first:
                                    filt(n + 1, 0 if last else i + 1, follows, (tap if first else 1,))
                                if tap == 2:
                                    variance(n + 1)
                            after = None if last else following(ddf, more) if last_but_one else ddf
                            if tap == TAPS - 1 and last_but_one and ddf == 2 and more:
                                pe.wait_ge(x_summed, (im + 1) * PIECES + 1)
                            if tap == TAPS - 1 and after is not None:
                                filt(n + 2, 0 if last_but_one else i + 2, after, (0,))
                            if ddf and not first:
                                accumulate(i - 1, 1 - par, tap)
                            if ddf == 0 and 1 <= tap < 7 and started(i, 3):
                                half, blocks = ((0, (1, 2)), (0, (3,)), (0, (4, 5)),
                                                (1, (0, 1)), (1, (2, 3)), (1, (4, 5)))[tap - 1]
                                group(i - 2, half, blocks)
                            if ddf == 0 and tap == 7 and started(i, 2):
                                for p, count in ((par, pair), (1 - par, pair if par == 0 else pair + 1)):
                                    pe.wait_ge(paired[p], (im * (TILES // 2) + count) * (2 * HALVES * 16) + PRIMED)
                                group(i - 1, 0, (0,))
                            if ddf == 0 and tap == 8 and last:
                                group(i - 1, 0, (1, 2))

                    tiles(pe, step, 2 if ddf else 4, opened=(ddf == 0))
                    if ddf == 0:
                        group(CONV_GROUPS - 2, 0, (3, 4, 5))
                        group(CONV_GROUPS - 2, 1)
                        pe.wait_ge(paired[1], (im + 1) * (TILES // 2 * 2 * HALVES * 16) + PRIMED)
                        before = im * (2 * CONV_GROUPS) + half_groups(0) - 1
                        pe.wait_ge(conv_staged, before + PRIMED)
                        convolve(HPAIRS - 1, 2, psum_rows(acc, 0, 2)).then_inc(conv_ready, 1)
                        pe.wait_ge(conv_staged, before + 1 + PRIMED)
                        pe.wait_ge(edge_zeroed, im + 1)
                        convolve(0, 1, psum_rows(acc, 2, 1))
                        convolve(PAIRS - 1, 1, psum_rows(acc, 3, 1)).then_inc(conv_ready, 1)
                        group(CONV_GROUPS - 1, 0)
                        group(CONV_GROUPS - 1, 1, (0, 1, 2, 3))
                        pe.wait_ge(conv_stored, im * STORES + stores(CONV_GROUPS - 1) + PRIMED)
                        filt(base + TILES, 0, 1)
                        group(CONV_GROUPS - 1, 1, (4,))
                        variance(base + TILES)
                        group(CONV_GROUPS - 1, 1, (5,))
                    if ddf == 2 and more:
                        def last_sum(tap, accumulate=accumulate, base=base):
                            if tap == 1:
                                pe.wait_ge(product_ready, (base + TILES) * TAPS + PRIMED)
                            for turn in ((), (1, 3), (4,), (5,), (6,), (7,), (), (), ())[tap]:
                                accumulate(TILES - 1, 1, turn)

                        open_image(im + 1, last_sum)
                    elif ddf:
                        pe.wait_ge(product_ready, (base + TILES) * TAPS + PRIMED)
                        for tap in range(TAPS):
                            accumulate(TILES - 1, 1, tap)

            pe.wait_ge(x_summed, 1)
            filt(0, 0, 0)
            variance(0)
            open_image(0)
            with pe.Fori(0, IMAGES - 1) as im:
                image_body(im, True)
            image_body(IMAGES - 1, False)


def kernel(x, L0_conv_Ws, L0_conv_bs, L0_conv_W1, L0_conv_b1, L0_conv_W2, L0_conv_b2, L0_conv_std_ch,
           L0_conv_Wc, L0_conv_bc, L1_conv_sw1, L1_conv_sb1, L1_conv_sstd1, L1_conv_cw1_1, L1_conv_cb1_1,
           L1_conv_cw2_1, L1_conv_cb2_1, L1_conv_cstd1, L1_conv_sw2, L1_conv_sb2, L1_conv_sstd2,
           L1_conv_cw1_2, L1_conv_cb1_2, L1_conv_cw2_2, L1_conv_cb2_2, L1_conv_cstd2):
    import concourse.bacc as bacc
    from concourse.bass_utils import run_bass_kernel_spmd

    f32 = np.float32
    a = np.asarray
    wspatial = np.zeros((P, DDFS, TAPS), f32)
    bspatial = np.zeros((1, DDFS, TAPS), f32)
    w1 = np.zeros((P, DDFS, 32), f32)
    b1 = np.zeros((32 * DDFS, 1), f32)
    w2 = np.zeros((32 * DDFS, TAPS, C), f32)
    tabs = np.zeros((P, 3, DDFS, TAPS), f32)
    tabs[:, 2, 0, :] = STD_SPATIAL
    for d, (ws, bs, u1, c1, u2, c2, std) in enumerate((
            (L0_conv_Ws, L0_conv_bs, L0_conv_W1, L0_conv_b1, L0_conv_W2, L0_conv_b2, L0_conv_std_ch),
            (L1_conv_sw1, L1_conv_sb1, L1_conv_cw1_1, L1_conv_cb1_1, L1_conv_cw2_1, L1_conv_cb2_1, L1_conv_cstd1),
            (L1_conv_sw2, L1_conv_sb2, L1_conv_cw1_2, L1_conv_cb1_2, L1_conv_cw2_2, L1_conv_cb2_2, L1_conv_cstd2))):
        bspatial[0, d] = a(bs)
        b1[32 * d:32 * d + MID, 0] = a(c1)
        w2[32 * d:32 * d + MID] = a(u2).reshape(C, TAPS, MID).transpose(2, 1, 0)
        for half in range(HALVES):
            h = slice(half * C, (half + 1) * C)
            wspatial[h, d] = a(ws).T
            w1[h, d, :MID] = a(u1).T
            tabs[h, 0, d] = a(c2).reshape(C, TAPS)
            tabs[h, 1, d] = a(std).reshape(C, TAPS)
    tabs[:, 2, 1, :] = a(L1_conv_sstd1)
    tabs[:, 2, 2, :] = a(L1_conv_sstd2)
    wconv = np.zeros((P, BLOCKS, P), f32)
    bconv = np.zeros((P, 1), f32)
    for t in range(2):
        bconv[t * C:(t + 1) * C, 0] = a(L0_conv_bc)
        for late in range(2):
            for s in range(2):
                du = 2 * late + s - t
                if 0 <= du < 3:
                    for dv in range(3):
                        wconv[s * C:(s + 1) * C, late * 3 + dv, t * C:(t + 1) * C] = a(L0_conv_Wc)[:, :, du, dv].T
    ident = np.eye(P, dtype=f32)
    wvar = np.zeros((P, P), f32)
    for chunk in range(2):
        for r in range(FILTERS, P // 2):
            wvar[chunk * 64 + r, chunk * 64 + r] = 1.0
    wcopy = np.zeros((P, TAPS, P), f32)
    masks = np.zeros((P, 4), f32)
    masks[:, 2] = EPS
    masks[:, 3] = TINY
    for chunk in range(2):
        for part in range(PARTS):
            masks[chunk * 64 + part * 18:chunk * 64 + part * 18 + 18, 0] = -1.0 if part > 0 else 0.0
            masks[chunk * 64 + part * 18:chunk * 64 + part * 18 + 18, 1] = -1.0 if part > 1 else 0.0
            for half in range(HALVES):
                r = chunk * 64 + part * 18 + half * TAPS
                wvar[r:r + TAPS, r:r + TAPS] = 1.0 / (TAPS - 1)
                for tap in range(TAPS):
                    wcopy[r + tap, tap, half * C:(half + 1) * C] = 1.0
    wcopy = wcopy.reshape(P, TAPS * P)

    arrays = {"x": np.ascontiguousarray(a(x)), "wspatial": wspatial, "bspatial": bspatial, "w1": w1, "b1": b1,
              "w2": w2, "tabs": tabs, "wconv": wconv, "bconv": bconv, "ident": ident, "wvar": wvar,
              "wcopy": wcopy, "masks": masks}
    nc = bacc.Bacc("TRN2", target_bir_lowering=False, num_devices=1)
    args = [nc.dram_tensor(f"in_{k}", v.shape, mybir.dt.from_np(v.dtype), kind="ExternalInput").ap()
            for k, v in arrays.items()]
    res = nc.dram_tensor("result_dram", (IMAGES, C, H, W), F32, kind="ExternalOutput").ap()
    ddf_stack_kernel(nc, *args, res)
    r = run_bass_kernel_spmd(nc, [{f"in_{k}": v for k, v in arrays.items()}], core_ids=[0])
    return r.results[0]["result_dram"]
```
